# Optimizing a Trainium2 kernel written in Bass

```python
import numpy as np
import jax
import jax.numpy as jnp

def _softmax(x, axis=-1):
    return jax.nn.softmax(x, axis=axis)

def _gelu(x):
    return jax.nn.gelu(x, approximate=True)

def _silu(x):
    return jax.nn.silu(x)

def _sigmoid(x):
    return jax.nn.sigmoid(x)

def _layernorm(x, axis=-1, eps=1e-05):
    m = jnp.mean(x, axis=axis, keepdims=True)
    v = jnp.var(x, axis=axis, keepdims=True)
    return (x - m) / jnp.sqrt(v + eps)

def _scatter_add(tgt, idx, src, axis=0):
    return tgt.at[idx].add(src)

def _segment_sum(src, seg, n):
    return jax.ops.segment_sum(src, seg, n)
kernel_name = 'mk_recurrent_d1_jaxref_r8_1de646'

def setup_inputs(seed: int=0):
    np.random.seed(seed)
    _w = jnp.asarray

    def _L0_attn_setup():
        import jax, jax.numpy as jnp
        import numpy as np
        import math
        B, S, D, H = (4, 256, 128, 16)
        DK = D // H
        key = jax.random.key(seed)
        ks = jax.random.split(key, 5)
        scale = 1.0 / math.sqrt(D)
        return {'x': jax.random.normal(ks[0], (B, S, D), dtype=jnp.float32), 'Wv': jax.random.normal(ks[1], (D, D), dtype=jnp.float32) * scale, 'bv': jax.random.normal(ks[2], (D,), dtype=jnp.float32) * scale, 'Wo': jax.random.normal(ks[3], (D, D), dtype=jnp.float32) * scale, 'bo': jax.random.normal(ks[4], (D,), dtype=jnp.float32) * scale}
    _L0_attn_in = _L0_attn_setup()

    def _L0_ffn_setup():
        import jax, jax.numpy as jnp
        import numpy as np
        E = 8
        TOP_K = 2
        LN_EPS = 1e-05

        def _layernorm(x, g, b):
            mu = jnp.mean(x, axis=-1, keepdims=True)
            var = jnp.var(x, axis=-1, keepdims=True)
            return (x - mu) * jax.lax.rsqrt(var + LN_EPS) * g + b
        key = jax.random.key(seed)
        ks = jax.random.split(key, 4)
        B, T, H, HF = (4, 256, 128, 256)
        s_in = 1.0 / np.sqrt(H)
        s_hid = 1.0 / np.sqrt(HF)
        return {'x': jax.random.normal(ks[0], (B, T, H), dtype=jnp.float32), 'ln_g': jnp.ones((H,), dtype=jnp.float32), 'ln_b': jnp.zeros((H,), dtype=jnp.float32), 'rW': jax.random.normal(ks[1], (H, E), dtype=jnp.float32) * s_in, 'rb': jnp.zeros((E,), dtype=jnp.float32), 'W1': jax.random.normal(ks[2], (E, H, HF), dtype=jnp.float32) * s_in, 'b1': jnp.zeros((E, HF), dtype=jnp.float32), 'W2': jax.random.normal(ks[3], (E, HF, H), dtype=jnp.float32) * s_hid, 'b2': jnp.zeros((E, H), dtype=jnp.float32)}
    _L0_ffn_in = _L0_ffn_setup()
    _d = {'L0_attn_x': _L0_attn_in['x'], 'L0_attn_Wv': _L0_attn_in['Wv'], 'L0_attn_bv': _L0_attn_in['bv'], 'L0_attn_Wo': _L0_attn_in['Wo'], 'L0_attn_bo': _L0_attn_in['bo'], 'L0_ffn_ln_g': _L0_ffn_in['ln_g'], 'L0_ffn_ln_b': _L0_ffn_in['ln_b'], 'L0_ffn_rW': _L0_ffn_in['rW'], 'L0_ffn_rb': _L0_ffn_in['rb'], 'L0_ffn_W1': _L0_ffn_in['W1'], 'L0_ffn_b1': _L0_ffn_in['b1'], 'L0_ffn_W2': _L0_ffn_in['W2'], 'L0_ffn_b2': _L0_ffn_in['b2']}
    _x0 = _d['L0_attn_x']
    _d['L0_attn_x'] = jax.random.normal(jax.random.fold_in(jax.random.key(seed), 1), (4, 1024, 128), dtype=_x0.dtype)
    del _x0
    return _d

def reference(L0_attn_x, L0_attn_Wv, L0_attn_bv, L0_attn_Wo, L0_attn_bo, L0_ffn_ln_g, L0_ffn_ln_b, L0_ffn_rW, L0_ffn_rb, L0_ffn_W1, L0_ffn_b1, L0_ffn_W2, L0_ffn_b2):

    def _L0_attn_ref(x, Wv, bv, Wo, bo):
        import jax, jax.numpy as jnp
        import numpy as np
        import math
        B, S, D, H = (4, 256, 128, 16)
        DK = D // H
        b, s, d = x.shape
        h, dk = (H, DK)
        p = jnp.einsum('bsd,ed->bse', x, Wv) + bv
        p = p.reshape(b, s, h, dk).transpose(0, 2, 1, 3)
        q = k = v = p
        scores = jnp.einsum('bhqd,bhkd->bhqk', q, k) / math.sqrt(dk)
        attn = jax.nn.softmax(scores, axis=-1)
        out = jnp.einsum('bhqk,bhkd->bhqd', attn, v)
        out = out.reshape(b, s, h * dk)
        return jnp.einsum('bsd,ed->bse', out, Wo) + bo

    def _L0_ffn_ref(x, ln_g, ln_b, rW, rb, W1, b1, W2, b2):
        import jax, jax.numpy as jnp
        import numpy as np
        E = 8
        TOP_K = 2
        LN_EPS = 1e-05

        def _layernorm(x, g, b):
            mu = jnp.mean(x, axis=-1, keepdims=True)
            var = jnp.var(x, axis=-1, keepdims=True)
            return (x - mu) * jax.lax.rsqrt(var + LN_EPS) * g + b
        z = _layernorm(x, ln_g, ln_b)
        logits = jnp.einsum('bth,he->bte', z, rW) + rb
        probs = jax.nn.softmax(logits, axis=-1)
        topv, topi = jax.lax.top_k(probs, TOP_K)
        mask = jnp.sum(jax.nn.one_hot(topi, E, dtype=probs.dtype) * topv[..., None], axis=-2)
        denom = jnp.maximum(jnp.sum(mask, axis=-1, keepdims=True), 1e-08)
        w = mask / denom
        hid = jax.nn.gelu(jnp.einsum('bth,ehf->btef', z, W1) + b1, approximate=False)
        outs = jnp.einsum('btef,efh->bteh', hid, W2) + b2
        mixed = jnp.sum(outs * w[..., None], axis=2)
        return x + mixed
    x = L0_attn_x
    xn = _layernorm(x, axis=-1)
    s = _L0_attn_ref(xn, L0_attn_Wv, L0_attn_bv, L0_attn_Wo, L0_attn_bo)
    g = _silu(_L0_ffn_ref(xn, L0_ffn_ln_g, L0_ffn_ln_b, L0_ffn_rW, L0_ffn_rb, L0_ffn_W1, L0_ffn_b1, L0_ffn_W2, L0_ffn_b2))
    x = x + s * g
    return x

_drawn_inputs = setup_inputs


def setup_inputs(seed=0):
    import zlib

    import numpy as np

    out = dict(_drawn_inputs(seed))
    spreads = {'L0_ffn_ln_g': (1.0, 0.2),
     'L0_ffn_ln_b': (0.0, 0.1),
     'L0_ffn_rb': (0.0, 0.1),
     'L0_ffn_b1': (0.0, 0.292),
     'L0_ffn_b2': (0.0, 0.1)}
    factors = {}
    for name, (base, spread) in spreads.items():
        noise = np.random.default_rng([zlib.crc32(name.encode()), seed]).standard_normal(out[name].shape)
        drawn = base * np.exp(spread * noise) if base else spread * noise
        out[name] = jnp.asarray(drawn.astype(out[name].dtype))
    for name, factor in factors.items():
        out[name] = (out[name] * factor).astype(out[name].dtype)
    return out
```

```python
from contextlib import ExitStack

import concourse.bass as bass
import numpy as np
from concourse import mybir

F32 = mybir.dt.float32
BF16 = mybir.dt.bfloat16
I32 = mybir.dt.int32
U32 = mybir.dt.uint32
ALU = mybir.AluOpType
ACT = mybir.ActivationFunctionType
X = mybir.AxisListType.X

P = 128
B, S, D = 4, 1024, 128
H = 16
DK = D // H
N = B * S
NT = N // P
BLK = 512
NB = N // BLK
TB = BLK // P
E = 8
HF = 256
FC = HF // P
EPS = 1e-5
HG = H // 4
KT = S // P
QH = S // BLK
NU = B * HG
US = QH * KT
QR = D // DK
RH = S // QR
UT = 4 * RH // P
PARTS = 3
PROWS = PARTS * PARTS * DK
MROW = 96
MPARTS = 2
KROWS = MROW + MPARTS
VW = DK + 1
VPAD = H * VW + 32 - VW
VSLOT = 3 * VW + 32
SCALE = float(DK) ** -0.5
M2_LIMIT = 400.0
M2_LIMIT_BITS = int(np.float32(M2_LIMIT).view(np.int32))
CREDIT = 2
PV_CREDIT = US + 1
ES = 4
KQ_LOADS = 4 * (1 + PARTS) + 1
LNC = 8


def build(nc, x, Wv, bv, Wo, bo, ln_g, ln_b, rW, rb, W1, b1, W2, b2, out):
    ctx = ExitStack()
    with ctx:
        def sb(name, shape, dt=F32):
            return ctx.enter_context(nc.sbuf_tensor(name, shape, dt))

        def sem(name):
            return ctx.enter_context(nc.semaphore(name))

        x_tok = sb("x_tok", [P, NT, D])
        xn_tok = sb("xn_tok", [P, NT, D])
        z0_tok = sb("z0_tok", [P, NT, D])
        zT = sb("zT", [P, N])
        pT = sb("pT", [P, 2, BLK])
        sqT = sb("sqT", [P, 2, BLK])
        parts = sb("parts", [P, 2, PARTS, BLK], BF16)
        v_tok = sb("v_tok", [P, NT, VPAD])
        w1_sb = sb("w1_sb", [P, E, HF])
        w2_sb = sb("w2_sb", [P, E, FC, D])
        hid = sb("hid", [P, 2, FC, BLK])
        exps = sb("exps", [P, ES, 4, BLK])
        k_ring = sb("k_ring", [P, 2, 4, S], BF16)
        q_ring = sb("q_ring", [P, 2, 4, S], BF16)
        acc = sb("acc", [P, TB, D])
        attn = sb("attn", [RH, 4, QR, DK])
        attnT = sb("attnT", [P, 4 * RH])
        act_dummy = sb("act_dummy", [1, 1])
        y_sb = sb("y_sb", [P, UT, D])
        ident = sb("ident", [P, P])
        ones = sb("ones", [1, H])
        head_sel = sb("head_sel", [P, H])
        before = sb("before", [P, E, E])
        wv_sb = sb("wv_sb", [P, D])
        wo_sb = sb("wo_sb", [P, D])
        wvT = sb("wvT", [P, D])
        woT = sb("woT", [P, D])
        rows = sb("rows", [E * FC + 3, P])
        cols = sb("cols", [P, E * FC + 3])
        bv_bc = sb("bv_bc", [P, D])
        bo_bc = sb("bo_bc", [P, D])
        rb_bc = sb("rb_bc", [P, E])
        rw_sb = sb("rw_sb", [P, E])
        b2_sb = sb("b2_sb", [E, D])
        stats = sb("stats", [P, LNC, 6])
        mv = sb("mv", [P, LNC, 2])
        veps = sb("veps", [P, LNC])
        sdev = sb("sdev", [P, LNC])
        rstd = sb("rstd", [P, LNC])
        lg = sb("lg", [P, NT, E])
        ex = sb("ex", [P, NT, E])
        rank = sb("rank", [P, NT, E])
        w_tok = sb("w_tok", [P, NT, E])
        red = sb("red", [P, NT])
        red2 = sb("red2", [P, NT])
        w_cur = sb("w_cur", [P, TB, E])
        wT = sb("wT", [E, BLK])
        max16 = sb("max16", [H, NB])
        max_head = sb("max_head", [H, 1])
        m2 = sb("m2", [1, 1])
        m2_col = sb("m2_col", [H, 1])
        rden = sb("rden", [RH, 2, 4, 4])
        xnT = exps[:, 2:4, :, :].rearrange("p a b n -> p (a b n)")
        n2T = exps[0:H, 0:2, :, :].rearrange("p a b n -> p (a b n)")
        m_parts = z0_tok[0:H, :, :].rearrange("p t d -> p (t d)").bitcast(BF16).rearrange("p (a n) -> p a n", a=MPARTS)
        kq_f32 = k_ring[:, :, :, :].rearrange("p a b n -> p (a b n)").bitcast(F32)
        cmp_gt = kq_f32[:, 0:NT * E * E].rearrange("p (t e j) -> p t e j", e=E, j=E)
        cmp_eq = kq_f32[:, NT * E * E:2 * NT * E * E].rearrange("p (t e j) -> p t e j", e=E, j=E)
        w1_flat = w1_sb[:, :, :].rearrange("p e f -> p (e f)")
        o_sb = w1_flat[:, 0:S]
        v_ring = w2_sb[:, :, :, :].rearrange("p e c d -> p (e c d)")[:, 0:2 * KT * VSLOT].rearrange(
            "p (a k v) -> p a k v", a=2, k=KT)

        row_max = zT[:, 0:NT * H * QH].rearrange("p (t h q) -> p t h q", h=H, q=QH)
        row_max2 = zT[:, NT * H * QH:NT * H * (QH + 1)].rearrange("p (t h) -> p t h", h=H)

        pair = [ctx.enter_context(nc.psum_tensor(f"pair{i}", [P, 2, BLK], F32)) for i in range(2)]
        bank_o = [ctx.enter_context(nc.psum_tensor(f"bank_o{i}", [P, BLK], F32)) for i in range(2)]
        bank_m = [ctx.enter_context(nc.psum_tensor(f"bank_m{i}", [P, BLK], F32)) for i in range(2)]

        CIRC = 2 * PARTS - 1
        p_dram = nc.dram_tensor("p_dram", [H, CIRC, DK, N], BF16)
        m_dram = nc.dram_tensor("m_dram", [MPARTS, H, N], BF16)

        x_in = [sem(f"x_in{c}") for c in range(NT // LNC)]
        small_in = sem("small_in")
        rows_in = sem("rows_in")
        w1_in = sem("w1_in")
        w2_in = sem("w2_in")
        consts_ready = sem("consts_ready")
        pool_chain = sem("pool_chain")
        dve_chain = sem("dve_chain")
        veps_ready = sem("veps_ready")
        sdev_ready = sem("sdev_ready")
        xn_ready = sem("xn_ready")
        z0_ready = sem("z0_ready")
        wt_tr = sem("wt_tr")
        wt_copied = sem("wt_copied")
        xT_tr = sem("xT_tr")
        xT_copied = sem("xT_copied")
        zT_tr = sem("zT_tr")
        zT_ready = sem("zT_ready")
        logits_done = sem("logits_done")
        p_mm = sem("p_mm")
        p_added = sem("p_added")
        pT_mm = sem("pT_mm")
        pT_copied = sem("pT_copied")
        sq_ready = sem("sq_ready")
        n2_mm = sem("n2_mm")
        n2_copied = sem("n2_copied")
        parts_ready = sem("parts_ready")
        parts_stored = [sem(f"parts_stored{i}") for i in range(2)]
        max16_ready = sem("max16_ready")
        max16_tr = sem("max16_tr")
        m2_ready = sem("m2_ready")
        m2_bc = sem("m2_bc")
        m2_col_ready = sem("m2_col_ready")
        m_ready = sem("m_ready")
        m_stored = sem("m_stored")
        router_d = sem("router_d")
        router_ex = sem("router_ex")
        router_done = sem("router_done")
        w_cur_ready = sem("w_cur_ready")
        w_tr = sem("w_tr")
        wT_ready = sem("wT_ready")
        bias_mm = sem("bias_mm")
        bias_used = sem("bias_used")
        up_mm = sem("up_mm")
        gelu_done = sem("gelu_done")
        down_mm = sem("down_mm")
        down_used = sem("down_used")
        gate_ready = sem("gate_ready")
        xg_ready = sem("xg_ready")
        ring_cleared = sem("ring_cleared")
        kq_in = [sem(f"kq_in{i}") for i in range(2)]
        v_ready = sem("v_ready")
        scores_done = sem("scores_done")
        exp_done = sem("exp_done")
        pv_done = sem("pv_done")
        o_copied = sem("o_copied")
        o_tr = sem("o_tr")
        attn_ready = sem("attn_ready")
        attn_tr = sem("attn_tr")
        attnT_ready = sem("attnT_ready")
        proj_done = sem("proj_done")
        y_ready = sem("y_ready")
        y_stored = sem("y_stored")
        y_free = sem("y_free")
        exact_in = sem("exact_in")
        exact_mm = sem("exact_mm")
        exact_max = sem("exact_max")
        exact_max2 = sem("exact_max2")
        exact_tr = sem("exact_tr")
        exact_neg = sem("exact_neg")
        exact_hi = sem("exact_hi")
        exact_split = sem("exact_split")
        pe_gate = sem("pe_gate")
        act_dummy_ready = sem("act_dummy_ready")

        x_v = x.rearrange("b s d -> (b s) d").rearrange("(t p) d -> p t d", p=P)
        out_rows = out.rearrange("b s d -> (b s) d")

        def chained(eng, semaphore):
            count = [0]

            def link(ins):
                count[0] += 1
                ins.then_inc(semaphore, 1)
                eng.wait_ge(semaphore, count[0])
            return link, count

        block = ctx.enter_context(nc.Block())

        @block.sync
        def _(sp):
            for c in range(NT // LNC):
                sp.dma_start(x_tok[:, c * LNC:(c + 1) * LNC, :], x_v[:, c * LNC:(c + 1) * LNC, :]).then_inc(x_in[c], 16)
            R = E * FC
            sp.dma_start(rows[0:R, :], b1.rearrange("e (c f) -> (e c) f", c=FC)).then_inc(rows_in, 16)
            sp.dma_start(rows[R:R + 1, :], ln_g.rearrange("(a d) -> a d", a=1)).then_inc(rows_in, 16)
            sp.dma_start(rows[R + 1:R + 2, :], ln_b.rearrange("(a d) -> a d", a=1)).then_inc(rows_in, 16)
            sp.dma_start(rows[R + 2:R + 3, :], bv.rearrange("(a d) -> a d", a=1)).then_inc(rows_in, 16)
            sp.dma_start(wv_sb[:, :], Wv).then_inc(rows_in, 16)
            sp.dma_start(wo_sb[:, :], Wo).then_inc(rows_in, 16)
            sp.dma_start(rw_sb[:, :], rW).then_inc(small_in, 16)
            sp.dma_start(bv_bc[:, :], bv.rearrange("(a d) -> a d", a=1).broadcast_to([P, D])).then_inc(small_in, 16)
            sp.dma_start(bo_bc[:, :], bo.rearrange("(a d) -> a d", a=1).broadcast_to([P, D])).then_inc(small_in, 16)
            sp.dma_start(rb_bc[:, :], rb.rearrange("(a d) -> a d", a=1).broadcast_to([P, E])).then_inc(small_in, 16)
            sp.dma_start(b2_sb[:, :], b2).then_inc(small_in, 16)
            sp.dma_start(w1_sb[:, :, :], W1.rearrange("e h f -> h e f")).then_inc(w1_in, 16)
            for e in range(E):
                sp.dma_start(w2_sb[:, e, :, :], W2[e].rearrange("(c p) h -> p c h", p=P)).then_inc(w2_in, 16)
            for g in range(NB):
                sp.wait_ge(parts_ready, g + 1)
                for blk in range(CIRC):
                    sp.dma_start(p_dram[:, blk, :, g * BLK:(g + 1) * BLK],
                                 parts[:, g % 2, blk % PARTS, :]).then_inc(parts_stored[g % 2], 16)
            sp.wait_ge(m_ready, 1)
            sp.dma_start(m_dram[:, :, :].rearrange("a h n -> h a n"), m_parts).then_inc(m_stored, 16)
            for i in range(2):
                sp.wait_ge(parts_stored[i], 16 * CIRC * NB // 2)
            sp.wait_ge(m_stored, 16)
            sp.wait_ge(ring_cleared, 1)

            def load_heads(w, i, slot, loaded):
                for j in range(4):
                    head = p_dram[bass.ds((w % 2) * 8 + (4 * i + j), 1), :, :, bass.ds((w // 2) * S, S)].rearrange(
                        "h a d n -> (h a d) n")
                    sp.dma_start(k_ring[0:PROWS, slot, j, :],
                                 head[0:PARTS * DK, :].unsqueeze(0).broadcast_to([PARTS, PARTS * DK, S])).then_inc(loaded, 16)
                    for c in range(PARTS):
                        sp.dma_start(q_ring[c * PARTS * DK:(c + 1) * PARTS * DK, slot, j, :],
                                     head[c * DK:(c + PARTS) * DK, :]).then_inc(loaded, 16)

            sp.wait_ge(m2_ready, 1)
            m2_bits = sp.value_load(m2[0:1, 0:1].bitcast(I32))
            with sp.If(m2_bits > M2_LIMIT_BITS):
                with sp.Fori(0, NU // 2) as w:
                    for i in range(2):
                        sp.wait_ge(exact_mm, (w * 2 + i) * US * 2 + 1)
                        load_heads(w, i, 0, exact_in)
                sp.wait_ge(exact_mm, NU * US * 2 + 1)
                sp.wait_ge(exact_split, 1)
                sp.dma_start(m_dram[:, :, :].rearrange("a h n -> h a n"), m_parts).then_inc(m_stored, 16)
                sp.wait_ge(m_stored, 32)

            with sp.Fori(0, NU // 2) as w:
                for i in range(2):
                    sp.wait_ge(pv_done, (w * 2 + i - 1) * US + PV_CREDIT)
                    load_heads(w, i, i, kq_in[i])
                    sp.dma_start(q_ring[MROW:KROWS, i, :, :],
                                 m_dram[:, bass.ds((w % 2) * 8 + 4 * i, 4), bass.ds((w // 2) * S, S)]).then_inc(kq_in[i], 16)

        @block.gpsimd
        def _(pool):
            link, count = chained(pool, pool_chain)
            pool.memset(ident[:, :], 0.0).then_inc(pool_chain, 1)
            pool.memset(head_sel[:, :], 1.0).then_inc(pool_chain, 1)
            pool.memset(before[:, :, :], 1.0).then_inc(pool_chain, 1)
            count[0] += 3
            pool.wait_ge(pool_chain, count[0])
            pool.affine_select(out=ident[:, :], in_=ident[:, :], compare_op=ALU.not_equal, fill=1.0, base=0,
                               pattern=[[-1, P]], channel_multiplier=1).then_inc(consts_ready, 1)
            link(pool.affine_select(out=head_sel[:, :], in_=head_sel[:, :], compare_op=ALU.is_ge, fill=0.0, base=0,
                                    pattern=[[-DK, H]], channel_multiplier=1))
            pool.affine_select(out=head_sel[:, :], in_=head_sel[:, :], compare_op=ALU.is_ge, fill=0.0, base=DK - 1,
                               pattern=[[DK, H]], channel_multiplier=-1).then_inc(consts_ready, 1)
            pool.affine_select(out=before[:, :, :], in_=before[:, :, :], compare_op=ALU.is_gt, fill=0.0, base=0,
                               pattern=[[1, E], [-1, E]], channel_multiplier=0).then_inc(consts_ready, 1)
            pool.memset(ones[:, :], 1.0).then_inc(consts_ready, 1)
            pool.memset(v_tok[:, :, H * VW:VPAD], 0.0)
            v_heads = v_tok[:, :, 0:H * VW].rearrange("p t (h v) -> p t h v", v=VW)
            link(pool.memset(v_heads[:, :, :, DK], 1.0))
            for g in range(NB):
                pool.wait_ge(pT_copied, g + 1)
                if g >= 2:
                    pool.wait_ge(parts_stored[g % 2], 16 * CIRC * (g // 2))
                src = pT[:, g % 2, :]
                link(pool.tensor_copy(parts[:, g % 2, 0, :], src))
                link(pool.tensor_tensor(src, src, parts[:, g % 2, 0, :], ALU.subtract))
                link(pool.tensor_copy(parts[:, g % 2, 1, :], src))
                pool.tensor_tensor(parts[:, g % 2, 2, :], src, parts[:, g % 2, 1, :], ALU.subtract).then_inc(parts_ready, 1)
            pool.wait_ge(n2_copied, NB)
            pool.wait_ge(m2_col_ready, 1)
            link(pool.tensor_scalar(n2T, n2T, m2_col[:, 0:1], -0.5, ALU.add, ALU.mult))
            pool.wait_ge(zT_tr, NB)
            link(pool.tensor_copy(m_parts[:, 0, :], n2T))
            pool.tensor_tensor(m_parts[:, 1, :], n2T, m_parts[:, 0, :], ALU.subtract).then_inc(m_ready, 1)
            pool.wait_ge(router_done, 1)
            pool.memset(q_ring[:, :, :, :].rearrange("p a b n -> p (a b n)").bitcast(U32), 0)
            link(pool.memset(k_ring[:, :, :, :].rearrange("p a b n -> p (a b n)").bitcast(U32), 0))
            pool.memset(k_ring[MROW:KROWS, :, :, :], 1.0).then_inc(ring_cleared, 1)
            pool.wait_ge(ring_cleared, 1)

            def load_values(w, i):
                pool.tensor_copy(v_ring[:, i, :, :],
                                 v_tok[:, bass.ds((w // 2) * KT, KT), bass.ds((w % 2) * (8 * VW) + 4 * VW * i, VSLOT)]
                                 ).then_inc(v_ready, 1)

            def store(w, i):
                pool.wait_ge(y_ready, w * 2 + i + 2)
                pool.dma_start(out_rows[bass.ds((w * 2 + i) * UT * P, UT * P), :].rearrange("(t p) d -> p t d", p=P),
                               y_sb[:, :, :]).then_inc(y_stored, 16)
                pool.wait_ge(y_stored, (w * 2 + i + 1) * 16)
                pool.sem_inc(y_free, 1)

            pool.wait_ge(p_added, NB)
            pool.wait_ge(down_mm, NB * E + CREDIT)
            def step(w, first):
                for i in range(2):
                    pool.wait_ge(pv_done, (w * 2 + i - 1) * US + PV_CREDIT)
                    load_values(w, i)
                    if i == 1:
                        store(w, 0)
                    elif not first:
                        store(w - 1, 1)

            step(0, True)
            with pool.Fori(1, NU // 2) as w:
                step(w, False)
            store(NU // 2 - 1, 1)

        @block.scalar
        def _(act):
            def deviations(c):
                for i in range(2 * c, 2 * c + 2):
                    act.wait_ge(veps_ready, i + 1)
                    nc.scalar.activation(sdev[:, :], veps[:, :], ACT.Sqrt).then_inc(sdev_ready, 1)

            deviations(0)
            act.wait_ge(wt_tr, 1)
            nc.scalar.copy(wvT[:, :], bank_m[0][:, 0:D])
            nc.scalar.copy(woT[:, :], bank_m[0][:, D:2 * D])
            nc.scalar.copy(cols[:, :], bank_m[0][:, 2 * D:2 * D + E * FC + 3]).then_inc(wt_copied, 1)
            act.wait_ge(wt_copied, 1)
            bv_col = cols[:, E * FC + 2:E * FC + 3]
            for g in range(NB):
                if g % (LNC // TB) == 0 and g // (LNC // TB) + 1 < NT // LNC:
                    deviations(g // (LNC // TB) + 1)
                act.wait_ge(xT_tr, g + 1)
                nc.scalar.copy(xnT[:, g * BLK:(g + 1) * BLK], bank_o[g % 2][:, :]).then_inc(xT_copied, 1)
                act.wait_ge(pT_mm, g + 1)
                if g >= 2:
                    act.wait_ge(parts_ready, g - 1)
                    act.wait_ge(n2_mm, g - 1)
                nc.scalar.activation(sqT[:, g % 2, :], pair[1][:, 1, :], ACT.Square, bias=bv_col).then_inc(sq_ready, 1)
                nc.scalar.activation(pT[:, g % 2, :], pair[1][:, 1, :], ACT.Identity, bias=bv_col).then_inc(pT_copied, 1)
                act.wait_ge(n2_mm, g + 1)
                nc.scalar.copy(n2T[:, g * BLK:(g + 1) * BLK], bank_o[g % 2][0:H, :]).then_inc(n2_copied, 1)
            act.wait_ge(router_d, 1)
            nc.scalar.activation(ex[:, :, :], lg[:, :, :], ACT.Exp).then_inc(router_ex, 1)
            nc.scalar.activation(act_dummy[:, :], ones[:, 0:1], ACT.Gelu).then_inc(act_dummy_ready, 1)
            with act.Fori(0, NB) as u:
                for e in range(E):
                    if e == 1:
                        act.wait_ge(w_tr, u + 1)
                        nc.scalar.copy(wT[:, :], bank_m[0][0:E, :]).then_inc(wT_ready, 1)
                    for c in range(FC):
                        act.wait_ge(up_mm, (u * E + e) * FC + c + 1)
                        act.wait_ge(down_mm, u * E + e - 1 + CREDIT)
                        nc.scalar.activation(hid[:, e % 2, c, :], pair[e % 2][:, c, :], ACT.Gelu,
                                             bias=cols[:, e * FC + c:e * FC + c + 1]).then_inc(gelu_done, 1)
            act.wait_ge(down_used, NB * E + CREDIT)
            for c in range(4):
                part = xn_tok[:, c * NT // 4:(c + 1) * NT // 4, :]
                nc.scalar.activation(part, part, ACT.Silu).then_inc(gate_ready, 1)
            act.wait_ge(act_dummy_ready, 1)
            nc.scalar.activation(act_dummy[:, :], act_dummy[:, :], ACT.Exp)
            with act.Fori(0, NU // 2) as w:
                for i in range(2):
                    for k in range(US):
                        for half in range(2):
                            act.wait_ge(scores_done, ((w * 2 + i) * US + k) * 2 + half + 1)
                            if half == 0:
                                act.wait_ge(pv_done, (w * 2 + i) * US + k + 1 - ES + PV_CREDIT)
                            nc.scalar.activation(exps[:, k % ES, 2 * half:2 * half + 2, :], pair[half][:, :, :], ACT.Exp,
                                                 scale=SCALE).then_inc(exp_done, 1)

        @block.vector
        def _(dve):
            link, count = chained(dve, dve_chain)

            def norm(src, dst, c, i, ready):
                for t in range(LNC):
                    ins = nc.vector.bn_stats(stats[:, t, :], src[:, c * LNC + t, :])
                link(ins)
                for t in range(LNC):
                    ins = nc.vector.bn_aggr(mv[:, t, :], stats[:, t, :])
                link(ins)
                nc.vector.tensor_scalar(veps[:, :], mv[:, :, 1], EPS, None, ALU.add).then_inc(veps_ready, 1)
                dve.wait_ge(sdev_ready, i + 1)
                link(nc.vector.reciprocal(rstd[:, :], sdev[:, :]))
                for t in range(LNC):
                    ins = nc.vector.tensor_scalar(dst[:, c * LNC + t, :], src[:, c * LNC + t, :], mv[:, t, 0:1],
                                                  rstd[:, t:t + 1], ALU.subtract, ALU.mult)
                ins.then_inc(ready, 1)

            GC = NT // LNC
            g_col = cols[:, E * FC:E * FC + 1]
            b_col = cols[:, E * FC + 1:E * FC + 2]
            for c in range(GC + 1):
                if c < GC:
                    dve.wait_ge(x_in[c], 16)
                    norm(x_tok, xn_tok, c, 2 * c, xn_ready)
                    dve.wait_ge(xn_ready, c + 1)
                    norm(xn_tok, z0_tok, c, 2 * c + 1, z0_ready)
                if c == 0:
                    dve.wait_ge(wt_copied, 1)
                    dve.wait_ge(small_in, 16 * 5)
                    continue
                for g in range((c - 1) * LNC // TB, c * LNC // TB):
                    dve.wait_ge(zT_tr, g + 1)
                    nc.vector.tensor_scalar(zT[:, g * BLK:(g + 1) * BLK], bank_m[g % 2][:, :], g_col, b_col,
                                            ALU.mult, ALU.add).then_inc(zT_ready, 1)
                    dve.wait_ge(p_mm, g + 1)
                    v_heads = v_tok[:, g * TB:(g + 1) * TB, 0:H * VW].rearrange("p t (h v) -> p t h v", v=VW)
                    for t in range(TB):
                        ins = nc.vector.tensor_tensor(v_heads[:, t, :, 0:DK],
                                                      pair[0][:, g % 2, t * D:(t + 1) * D].rearrange("p (h d) -> p h d", d=DK),
                                                      bv_bc[:, :].rearrange("p (h d) -> p h d", d=DK), ALU.add)
                    ins.then_inc(p_added, 1)
                    dve.wait_ge(n2_copied, g + 1)
                    nc.vector.tensor_reduce(max16[:, g:g + 1], n2T[:, g * BLK:(g + 1) * BLK], X, ALU.max).then_inc(max16_ready, 1)
            dve.wait_ge(max16_ready, NB)
            nc.vector.tensor_reduce(max_head[:, :], max16[:, :], X, ALU.max).then_inc(max16_ready, 1)
            dve.wait_ge(max16_tr, 1)
            nc.vector.tensor_reduce(m2[:, :], bank_m[0][0:1, 0:H], X, ALU.max).then_inc(m2_ready, 1)
            dve.wait_ge(m2_bc, 1)
            nc.vector.tensor_copy(m2_col[:, :], bank_m[1][0:H, 0:1]).then_inc(m2_col_ready, 1)
            dve.wait_ge(logits_done, 1)
            link(nc.vector.tensor_tensor(lg[:, :, :], pair[1][:, 0, 0:NT * E].rearrange("p (t e) -> p t e", e=E),
                                         rb_bc[:, :].unsqueeze(1).broadcast_to([P, NT, E]), ALU.add))
            link(nc.vector.tensor_reduce(red[:, :], lg[:, :, :], X, ALU.max))
            nc.vector.tensor_tensor(lg[:, :, :], lg[:, :, :], red[:, :].unsqueeze(2).broadcast_to([P, NT, E]),
                                    ALU.subtract).then_inc(router_d, 1)
            dve.wait_ge(router_d, 1)
            other = lg[:, :, :].unsqueeze(2).broadcast_to([P, NT, E, E])
            own = lg[:, :, :].unsqueeze(3).broadcast_to([P, NT, E, E])
            nc.vector.tensor_tensor(cmp_gt, other, own, ALU.is_gt)
            link(nc.vector.tensor_tensor(cmp_eq, other, own, ALU.is_equal))
            dve.wait_ge(consts_ready, 4)
            link(nc.vector.tensor_tensor(cmp_eq, cmp_eq, before[:, :, :].unsqueeze(1).broadcast_to([P, NT, E, E]), ALU.mult))
            link(nc.vector.tensor_tensor(cmp_gt, cmp_gt, cmp_eq, ALU.add))
            link(nc.vector.tensor_reduce(rank[:, :, :], cmp_gt, X, ALU.add))
            dve.wait_ge(router_ex, 1)
            link(nc.vector.tensor_reduce(red[:, :], ex[:, :, :], X, ALU.add))
            link(nc.vector.reciprocal(red2[:, :], red[:, :]))
            link(nc.vector.tensor_tensor(ex[:, :, :], ex[:, :, :], red2[:, :].unsqueeze(2).broadcast_to([P, NT, E]), ALU.mult))
            link(nc.vector.scalar_tensor_tensor(out=ex[:, :, :], in0=rank[:, :, :], scalar=1.5, in1=ex[:, :, :],
                                                op0=ALU.is_lt, op1=ALU.mult))
            link(nc.vector.tensor_reduce(red[:, :], ex[:, :, :], X, ALU.add))
            link(nc.vector.tensor_scalar(red[:, :], red[:, :], 1e-8, None, ALU.max))
            link(nc.vector.reciprocal(red2[:, :], red[:, :]))
            nc.vector.tensor_tensor(w_tok[:, :, :], ex[:, :, :], red2[:, :].unsqueeze(2).broadcast_to([P, NT, E]),
                                    ALU.mult).then_inc(router_done, 1)
            dve.wait_ge(router_done, 1)
            base = count[0]
            with dve.Fori(0, NB) as u:
                dve.wait_ge(down_used, u * E + CREDIT)
                nc.vector.tensor_copy(w_cur[:, :, :], w_tok[:, bass.ds(u * TB, TB), :]).then_inc(w_cur_ready, 1)
                dve.wait_ge(bias_mm, u + 1)
                nc.vector.tensor_tensor(acc[:, :, :], bank_m[1][:, :].rearrange("p (t d) -> p t d", t=TB),
                                        xn_tok[:, bass.ds(u * TB, TB), :], ALU.add).then_inc(dve_chain, 1)
                dve.wait_ge(w_cur_ready, u + 1)
                for e in range(E):
                    dve.wait_ge(down_mm, u * E + e + 1 + CREDIT)
                    if e == 0:
                        dve.wait_ge(dve_chain, u + base + 1)
                    else:
                        dve.wait_ge(down_used, u * E + e + CREDIT)
                    for t in range(TB):
                        into = acc[:, t, :] if e < E - 1 else xn_tok[:, bass.ds(u * TB + t, 1), :].rearrange("p a d -> p (a d)")
                        ins = nc.vector.scalar_tensor_tensor(
                            out=into, in0=bank_o[e % 2][:, t * D:(t + 1) * D],
                            scalar=w_cur[:, t, e:e + 1], in1=acc[:, t, :], op0=ALU.mult, op1=ALU.add)
                    ins.then_inc(down_used, 1)
            link2_base = base + NB
            for c in range(4):
                gate = xn_tok[:, c * NT // 4:(c + 1) * NT // 4, :]
                into = x_tok[:, c * NT // 4:(c + 1) * NT // 4, :]
                tmp = zT[:, c * N // 4:(c + 1) * N // 4].rearrange("p (t d) -> p t d", d=D)
                dve.wait_ge(gate_ready, c + 1)
                nc.vector.tensor_tensor(tmp, gate, bo_bc[:, :].unsqueeze(1).broadcast_to([P, NT // 4, D]),
                                        ALU.mult).then_inc(dve_chain, 1)
                dve.wait_ge(dve_chain, link2_base + 2 * c + 1)
                nc.vector.tensor_tensor(into, into, tmp, ALU.add).then_inc(dve_chain, 1)
                dve.wait_ge(dve_chain, link2_base + 2 * c + 2)
            base2 = link2_base + 8
            m2_bits = dve.value_load(m2[0:1, 0:1].bitcast(I32))
            with dve.If(m2_bits > M2_LIMIT_BITS):
                with dve.Fori(0, NU // 2) as w:
                    for i in range(2):
                        for k in range(US):
                            qh, kt = divmod(k, KT)
                            for half in range(2):
                                step = ((w * 2 + i) * US + k) * 2 + half
                                dve.wait_ge(exact_mm, step + 2)
                                into = row_max[:, bass.ds((w // 2) * KT + kt, 1), bass.ds((w % 2) * 8 + (4 * i + 2 * half), 2), qh]
                                nc.vector.tensor_reduce(into.rearrange("p t h -> p (t h)"), pair[half][:, :, :], X,
                                                        ALU.max).then_inc(exact_max, 1)
                dve.wait_ge(exact_max, NU * US * 2 + CREDIT)
                nc.vector.tensor_reduce(row_max2, row_max, X, ALU.max).then_inc(exact_max2, 1)
                dve.wait_ge(m_ready, 1)
                for g in range(NB):
                    dve.wait_ge(exact_tr, g + 1)
                    nc.vector.tensor_scalar(n2T[:, g * BLK:(g + 1) * BLK], bank_m[g % 2][0:H, :], -1.0, None,
                                            ALU.mult).then_inc(exact_neg, 1)
                dve.wait_ge(exact_neg, NB)
                dve.wait_ge(m_stored, 16)
                nc.vector.tensor_copy(m_parts[:, 0, :], n2T).then_inc(exact_hi, 1)
                dve.wait_ge(exact_hi, 1)
                nc.vector.tensor_tensor(m_parts[:, 1, :], n2T, m_parts[:, 0, :], ALU.subtract).then_inc(exact_split, 1)
            per_unit = QR // 4 + 1
            with dve.Fori(0, NU // 2) as w:
                for i in range(2):
                    n = w * 2 + i
                    for qh in range(QH):
                        dve.wait_ge(pv_done, n * US + (qh + 1) * KT + PV_CREDIT)
                        nc.vector.tensor_copy(o_sb[:, qh * BLK:(qh + 1) * BLK], bank_o[qh][:, :]).then_inc(o_copied, 1)
                    for r in range(QR // 4):
                        dve.wait_ge(o_tr, n * (QR // 4) + r + 1)
                        o_rows = bank_m[r % 2][0:RH, :].rearrange("p (q j v) -> p q j v", q=4, j=4)
                        nc.vector.reciprocal(rden[:, r % 2, :, :], o_rows[:, :, :, DK]).then_inc(dve_chain, 1)
                        dve.wait_ge(dve_chain, n * per_unit + base2 + r + 1)
                        nc.vector.tensor_tensor(attn[:, :, 4 * r:4 * r + 4, :].rearrange("p j q d -> p q j d"),
                                                o_rows[:, :, :, 0:DK], rden[:, r % 2, :, :].unsqueeze(3).broadcast_to([RH, 4, 4, DK]),
                                                ALU.mult).then_inc(attn_ready, 1)
                    dve.wait_ge(attn_tr, n + 1)
                    nc.vector.tensor_copy(attnT[:, :], bank_m[0][:, 0:4 * RH]).then_inc(attnT_ready, 1)
                    dve.wait_ge(proj_done, n + 1)
                    dve.wait_ge(y_free, n + 1)
                    nc.vector.tensor_tensor(y_sb[:, :, :], bank_m[1][:, 0:UT * D].rearrange("p (t d) -> p t d", t=UT),
                                            xn_tok[:, bass.ds(n * UT, UT), :], ALU.mult).then_inc(dve_chain, 1)
                    dve.wait_ge(dve_chain, n * per_unit + base2 + per_unit)
                    nc.vector.tensor_tensor(y_sb[:, :, :], y_sb[:, :, :], x_tok[:, bass.ds(n * UT, UT), :],
                                            ALU.add).then_inc(y_ready, 1)

        @block.tensor
        def _(pe):
            pe.sem_inc(down_mm, CREDIT)
            pe.sem_inc(down_used, CREDIT)
            pe.sem_inc(exp_done, CREDIT)
            pe.sem_inc(o_copied, CREDIT)
            pe.sem_inc(y_ready, 1)
            pe.sem_inc(y_free, 1)
            pe.sem_inc(exact_mm, 1)
            pe.sem_inc(exact_max, CREDIT)
            pe.sem_inc(pv_done, PV_CREDIT)
            pe.wait_ge(consts_ready, 4)
            pe.wait_ge(rows_in, 16 * 6)
            nc.tensor.transpose(bank_m[0][:, 0:D], wv_sb[:, :], ident[:, :])
            nc.tensor.transpose(bank_m[0][:, D:2 * D], wo_sb[:, :], ident[:, :])
            R = E * FC + 3
            nc.tensor.transpose(bank_m[0][:, 2 * D:2 * D + R], rows[:, :], ident[0:R, 0:R]).then_inc(wt_tr, 1)
            pe.wait_ge(wt_copied, 1)
            pe.wait_ge(small_in, 16 * 5)
            for g in range(NB):
                pe.wait_ge(xn_ready, g * TB // LNC + 1)
                if g >= 2:
                    pe.wait_ge(n2_copied, g - 1)
                for t in range(TB):
                    ins = nc.tensor.transpose(bank_o[g % 2][:, t * P:(t + 1) * P], xn_tok[:, g * TB + t, :], ident[:, :])
                ins.then_inc(xT_tr, 1)
                pe.wait_ge(z0_ready, g * TB // LNC + 1)
                if g >= 2:
                    pe.wait_ge(zT_ready, g - 1)
                for t in range(TB):
                    ins = nc.tensor.transpose(bank_m[g % 2][:, t * P:(t + 1) * P], z0_tok[:, g * TB + t, :], ident[:, :])
                ins.then_inc(zT_tr, 1)
                pe.wait_ge(xT_copied, g + 1)
                if g >= 1:
                    pe.wait_ge(pT_copied, g)
                nc.tensor.matmul(pair[1][:, 1, :], wvT[:, :], xnT[:, g * BLK:(g + 1) * BLK], start=True, stop=True).then_inc(pT_mm, 1)
                if g >= 2:
                    pe.wait_ge(p_added, g - 1)
                for t in range(TB):
                    tile = xnT[:, (g * TB + t) * P:(g * TB + t + 1) * P]
                    ins = nc.tensor.matmul(pair[0][:, g % 2, t * D:(t + 1) * D], tile, wvT[:, :], start=True, stop=True)
                ins.then_inc(p_mm, 1)
                pe.wait_ge(sq_ready, g + 1)
                nc.tensor.matmul(bank_o[g % 2][0:H, :], head_sel[:, :], sqT[:, g % 2, :], start=True, stop=True).then_inc(n2_mm, 1)
                pe.wait_ge(zT_ready, g + 1)
                for t in range(g * TB, (g + 1) * TB):
                    ins = nc.tensor.matmul(pair[1][:, 0, t * E:(t + 1) * E], zT[:, t * P:(t + 1) * P], rw_sb[:, :],
                                           start=True, stop=True)
            ins.then_inc(logits_done, 1)
            pe.wait_ge(max16_ready, NB + 1)
            nc.tensor.transpose(bank_m[0][0:1, 0:H], max_head[:, :], ident[0:H, 0:H]).then_inc(max16_tr, 1)
            pe.wait_ge(m2_ready, 1)
            nc.tensor.matmul(bank_m[1][0:H, 0:1], ones[:, :], m2[:, :], start=True, stop=True).then_inc(m2_bc, 1)
            pe.wait_ge(m2_col_ready, 1)
            pe.wait_ge(router_d, 1)
            pe.wait_ge(p_added, NB)
            pe.wait_ge(w1_in, 16)
            pe.wait_ge(w2_in, 16 * E)
            with pe.Fori(0, NB) as u:
                def up(e):
                    for c in range(FC):
                        nc.tensor.matmul(pair[e % 2][:, c, :], w1_sb[:, e, c * P:(c + 1) * P], zT[:, bass.ds(u * BLK, BLK)],
                                         start=True, stop=True).then_inc(up_mm, 1)

                def down(e):
                    pe.wait_ge(gelu_done, (u * E + e + 1) * FC)
                    pe.wait_ge(down_used, u * E + e - 1 + CREDIT)
                    for t in range(TB):
                        for c in range(FC):
                            ins = nc.tensor.matmul(bank_o[e % 2][:, t * D:(t + 1) * D], hid[:, e % 2, c, t * P:(t + 1) * P],
                                                   w2_sb[:, e, c, :], start=(c == 0), stop=(c == FC - 1))
                    ins.then_inc(down_mm, 1)

                up(0)
                pe.wait_ge(w_cur_ready, u + 1)
                for t in range(TB):
                    ins = nc.tensor.transpose(bank_m[0][0:E, t * P:(t + 1) * P], w_cur[:, t, :], ident[:, :])
                ins.then_inc(w_tr, 1)
                up(1)
                pe.wait_ge(wT_ready, u + 1)
                for t in range(TB):
                    ins = nc.tensor.matmul(bank_m[1][:, t * D:(t + 1) * D], wT[:, t * P:(t + 1) * P], b2_sb[:, :],
                                           start=True, stop=True)
                ins.then_inc(bias_mm, 1)
                for e in range(2, E):
                    down(e - 2)
                    up(e)
                down(E - 2)
                down(E - 1)
            pe.wait_ge(down_used, NB * E + CREDIT)
            m2_bits = pe.value_load(m2[0:1, 0:1].bitcast(I32))
            with pe.If(m2_bits > M2_LIMIT_BITS):
                with pe.Fori(0, NU // 2) as w:
                    for i in range(2):
                        pe.wait_ge(exact_in, (w * 2 + i + 1) * 16 * (KQ_LOADS - 1))
                        for k in range(US):
                            qh, kt = divmod(k, KT)
                            for half in range(2):
                                step = ((w * 2 + i) * US + k) * 2 + half
                                pe.wait_ge(exact_max, step - 1 + CREDIT)
                                for j in range(2 * half, 2 * half + 2):
                                    ins = nc.tensor.matmul(pair[half][:, j % 2, :], k_ring[0:PROWS, 0, j, kt * P:(kt + 1) * P],
                                                           q_ring[0:PROWS, 0, j, qh * BLK:(qh + 1) * BLK], start=True, stop=True)
                                ins.then_inc(exact_mm, 1)
                pe.wait_ge(exact_max2, 1)
                for g in range(NB):
                    if g >= 2:
                        pe.wait_ge(exact_neg, g - 1)
                    for t in range(TB):
                        ins = nc.tensor.transpose(bank_m[g % 2][0:H, t * P:(t + 1) * P], row_max2[:, g * TB + t, :], ident[:, :])
                    ins.then_inc(exact_tr, 1)
                pe.wait_ge(exact_split, 1)

            def scores(w, i, k, half):
                qh, kt = divmod(k, KT)
                n = w * 2 + i
                if k == 0 and half == 0:
                    pe.wait_ge(kq_in[i], (w + 1) * 16 * KQ_LOADS)
                pe.wait_ge(exp_done, (n * US + k) * 2 + half - 1 + CREDIT)
                for j in range(2 * half, 2 * half + 2):
                    ins = nc.tensor.matmul(pair[half][:, j % 2, :], k_ring[0:KROWS, i, j, kt * P:(kt + 1) * P],
                                           q_ring[0:KROWS, i, j, qh * BLK:(qh + 1) * BLK], start=True, stop=True)
                ins.then_inc(scores_done, 1)

            def values(w, i, k):
                qh, kt = divmod(k, KT)
                n = w * 2 + i
                pe.wait_ge(exp_done, (n * US + k + 1) * 2 + CREDIT)
                if k == 0:
                    pe.wait_ge(v_ready, n + 1)
                if kt == 0:
                    pe.wait_ge(o_copied, n * 2 + qh - 1 + CREDIT)
                for j in range(4):
                    ins = nc.tensor.matmul(bank_o[qh][32 * j:32 * j + 32, :], v_ring[:, i, kt, VW * j:VW * j + 32],
                                           exps[:, k % ES, j, :], start=(kt == 0), stop=(kt == KT - 1))
                ins.then_inc(pv_done, 1)

            FINISH = QR // 4 + 2

            def finish(w, i, step):
                n = w * 2 + i
                if step < QR // 4:
                    if step == 0:
                        pe.wait_ge(o_copied, n * 2 + 2 + CREDIT)
                        pe.wait_ge(y_ready, n + 1)
                    if step >= 2:
                        pe.wait_ge(attn_ready, n * (QR // 4) + step - 1)
                    pe.sem_inc(pe_gate, 1)
                    queries = o_sb.rearrange("p (r s) -> p s r", s=QR)
                    for q in range(4):
                        ins = nc.tensor.transpose(bank_m[step % 2][0:RH, q * P:(q + 1) * P], queries[:, 4 * step + q, :],
                                                  ident[:, :])
                    ins.then_inc(o_tr, 1)
                elif step == QR // 4:
                    pe.wait_ge(attn_ready, (n + 1) * (QR // 4))
                    pe.sem_inc(pe_gate, 1)
                    for j in range(4):
                        ins = nc.tensor.transpose(bank_m[0][:, j * RH:(j + 1) * RH],
                                                  attn[:, j, :, :].rearrange("p q d -> p (q d)"), ident[0:RH, 0:RH])
                    ins.then_inc(attn_tr, 1)
                else:
                    pe.wait_ge(attnT_ready, n + 1)
                    for t in range(UT):
                        ins = nc.tensor.matmul(bank_m[1][:, t * D:(t + 1) * D], attnT[:, t * P:(t + 1) * P], woT[:, :],
                                               start=True, stop=True)
                    ins.then_inc(proj_done, 1)

            def two_units(w, first):
                for g in range(2 * US):
                    i, k = divmod(g, US)
                    scores(w, i, k, 0)
                    if g >= VLAG:
                        values(w, *divmod(g - VLAG, US))
                    elif not first:
                        values(w - 1, 1, US + g - VLAG)
                    scores(w, i, k, 1)
                    if k - VLAG in FINISH_AT:
                        step = FINISH_AT.index(k - VLAG)
                        if i == 1:
                            finish(w, 0, step)
                        elif not first:
                            finish(w - 1, 1, step)

            VLAG = 2
            FINISH_AT = [1, 2, 3, 4, 6, 8]
            assert len(FINISH_AT) == FINISH
            two_units(0, True)
            with pe.Fori(1, NU // 2) as w:
                two_units(w, False)
            for k in range(US - VLAG, US):
                values(NU // 2 - 1, 1, k)
            for step in range(FINISH):
                finish(NU // 2 - 1, 1, step)


_INS = ['L0_attn_x', 'L0_attn_Wv', 'L0_attn_bv', 'L0_attn_Wo', 'L0_attn_bo', 'L0_ffn_ln_g', 'L0_ffn_ln_b', 'L0_ffn_rW',
        'L0_ffn_rb', 'L0_ffn_W1', 'L0_ffn_b1', 'L0_ffn_W2', 'L0_ffn_b2']


def kernel(**inputs):
    import numpy as _np
    import concourse.bacc as _bacc
    from concourse.bass_utils import run_bass_kernel_spmd as _run

    nc = _bacc.Bacc("TRN2", target_bir_lowering=False, num_devices=1)
    arrays, args = {}, []
    for name in _INS:
        a = _np.ascontiguousarray(inputs[name])
        arrays[f"in_{name}"] = a
        args.append(nc.dram_tensor(f"in_{name}", a.shape, mybir.dt.from_np(a.dtype), kind="ExternalInput").ap())
    result = nc.dram_tensor("out_x", (B, S, D), F32, kind="ExternalOutput").ap()
    build(nc, *args, result)
    r = _run(nc, [arrays], core_ids=[0])
    return r.results[0]["out_x"]
```

```python
from contextlib import ExitStack

import concourse.bass as bass
import numpy as np
from concourse import mybir

F32 = mybir.dt.float32
BF16 = mybir.dt.bfloat16
I32 = mybir.dt.int32
U32 = mybir.dt.uint32
ALU = mybir.AluOpType
ACT = mybir.ActivationFunctionType
X = mybir.AxisListType.X

P = 128
B, S, D = 4, 1024, 128
H = 16
DK = D // H
N = B * S
NT = N // P
BLK = 512
NB = N // BLK
TB = BLK // P
E = 8
HF = 256
FC = HF // P
EPS = 1e-5
HG = H // 4
KT = S // P
QH = S // BLK
NU = B * HG
US = QH * KT
QR = D // DK
RH = S // QR
UT = 4 * RH // P
PARTS = 3
PROWS = PARTS * PARTS * DK
MROW = 96
MPARTS = 2
KROWS = MROW + MPARTS
VW = DK + 1
VPAD = H * VW + 32 - VW
VSLOT = 3 * VW + 32
SCALE = float(DK) ** -0.5
RSQRT_SEED = 0x5F3759DF
NEWTON = 3
M2_LIMIT = 400.0
M2_LIMIT_BITS = int(np.float32(M2_LIMIT).view(np.int32))
CREDIT = 2
PV_CREDIT = US + 1
ES = 4
KQ_LOADS = 4 * (1 + PARTS) + 1
XC = 8


def build(nc, x, Wv, bv, Wo, bo, ln_g, ln_b, rW, rb, W1, b1, W2, b2, out):
    ctx = ExitStack()
    with ctx:
        def sb(name, shape, dt=F32):
            return ctx.enter_context(nc.sbuf_tensor(name, shape, dt))

        def sem(name):
            return ctx.enter_context(nc.semaphore(name))

        x_tok = sb("x_tok", [P, NT, D])
        xn_tok = sb("xn_tok", [P, NT, D])
        local = sb("local", [P, 9, BLK])
        scratch = sb("scratch", [P, N])
        pT = sb("pT", [P, 2, BLK])
        parts = sb("parts", [P, 2, PARTS, BLK], BF16)
        v_tok = sb("v_tok", [P, NT, VPAD])
        w1_sb = sb("w1_sb", [P, E, HF])
        w2_sb = sb("w2_sb", [P, E, FC, D])
        hid = sb("hid", [P, 2, FC, BLK])
        exps = sb("exps", [P, ES, 4, BLK])
        k_ring = sb("k_ring", [P, 2, 4, S], BF16)
        q_ring = sb("q_ring", [P, 2, 4, S], BF16)
        acc = sb("acc", [P, TB, D])
        attn = sb("attn", [RH, 4, QR, DK])
        attnT = sb("attnT", [P, 4 * RH])
        act_dummy = sb("act_dummy", [1, 1])
        y_sb = sb("y_sb", [P, UT, D])
        ident = sb("ident", [P, P])
        ones = sb("ones", [1, 1])
        head_sel = sb("head_sel", [P, H])
        before = sb("before", [P, E, E])
        wv_sb = sb("wv_sb", [P, D])
        wo_sb = sb("wo_sb", [P, D])
        wvT = sb("wvT", [P, D])
        woT = sb("woT", [P, D])
        rows = sb("rows", [E * FC + 3, P])
        cols = sb("cols", [P, E * FC + 3])
        bv_bc = sb("bv_bc", [P, D])
        bo_bc = sb("bo_bc", [P, D])
        rb_bc = sb("rb_bc", [P, E])
        rw_sb = sb("rw_sb", [P, E])
        b2_sb = sb("b2_sb", [E, D])
        stats = sb("stats", [P, TB, 6])
        mv = sb("mv", [P, TB, 2])
        veps = sb("veps", [P, TB])
        newton = sb("newton", [P, TB])
        rstd = sb("rstd", [P, TB])
        lg = sb("lg", [P, TB, E])
        ex = sb("ex", [P, TB, E])
        rank = sb("rank", [P, TB, E])
        red = sb("red", [P, TB])
        red2 = sb("red2", [P, TB])
        cmp_gt = sb("cmp_gt", [P, TB, E, E])
        cmp_eq = sb("cmp_eq", [P, TB, E, E])
        w_blk = sb("w_blk", [P, 2, TB, E])
        wT = sb("wT", [E, BLK])
        max_head = sb("max_head", [H, 1])
        m2 = sb("m2", [1, 1])
        rden = sb("rden", [RH, 2, 4, 4])
        xn_blk = local[:, 0:2, :].rearrange("p a (t d) -> p a t d", d=D)
        zT = local[:, 2:4, :]
        z0_blk = local[:, 4, :].rearrange("p (t d) -> p t d", d=D)
        xnT = local[:, 5, :]
        sqT = local[:, 6, :]
        n2T = exps[0:H, 0:2, :, :].rearrange("p a b n -> p (a b n)")
        m_half = local[0:H, 7, :]
        m_blk = local[0:H, 8, :].bitcast(BF16).rearrange("p (a n) -> p a n", a=MPARTS)
        w1_flat = w1_sb[:, :, :].rearrange("p e f -> p (e f)")
        o_sb = w1_flat[:, 0:S]
        v_ring = w2_sb[:, :, :, :].rearrange("p e c d -> p (e c d)")[:, 0:2 * KT * VSLOT].rearrange(
            "p (a k v) -> p a k v", a=2, k=KT)

        row_max = scratch[:, 0:NT * H * QH].rearrange("p (t h q) -> p t h q", h=H, q=QH)
        m_parts = scratch[0:H, :].bitcast(BF16).rearrange("p (a n) -> p a n", a=MPARTS)
        row_max2 = scratch[:, NT * H * QH:NT * H * (QH + 1)].rearrange("p (t h) -> p t h", h=H)

        pair = [ctx.enter_context(nc.psum_tensor(f"pair{i}", [P, 2, BLK], F32)) for i in range(2)]
        bank_o = [ctx.enter_context(nc.psum_tensor(f"bank_o{i}", [P, BLK], F32)) for i in range(2)]
        bank_m = [ctx.enter_context(nc.psum_tensor(f"bank_m{i}", [P, BLK], F32)) for i in range(2)]

        CIRC = 2 * PARTS - 1
        p_dram = nc.dram_tensor("p_dram", [H, CIRC, DK, N], BF16)
        m_dram = nc.dram_tensor("m_dram", [MPARTS, H, N], BF16)

        x_in = [sem(f"x_in{c}") for c in range(NT // XC)]
        small_in = sem("small_in")
        rows_in = sem("rows_in")
        w1_in = sem("w1_in")
        w2_in = sem("w2_in")
        consts_ready = sem("consts_ready")
        pool_chain = sem("pool_chain")
        dve_chain = sem("dve_chain")
        xn_ready = sem("xn_ready")
        z0_ready = sem("z0_ready")
        wt_tr = sem("wt_tr")
        wt_copied = sem("wt_copied")
        xT_tr = sem("xT_tr")
        xT_copied = sem("xT_copied")
        zT_tr = sem("zT_tr")
        zT_ready = sem("zT_ready")
        logits_mm = sem("logits_mm")
        logits_used = sem("logits_used")
        p_mm = sem("p_mm")
        p_added = sem("p_added")
        pT_mm = sem("pT_mm")
        pT_copied = sem("pT_copied")
        sq_ready = sem("sq_ready")
        n2_mm = sem("n2_mm")
        n2_copied = sem("n2_copied")
        parts_ready = sem("parts_ready")
        parts_stored = sem("parts_stored")
        parts_free = sem("parts_free")
        max_head_ready = sem("max_head_ready")
        max_head_tr = sem("max_head_tr")
        m2_ready = sem("m2_ready")
        m_ready = sem("m_ready")
        m_stored = sem("m_stored")
        router_d = sem("router_d")
        router_ex = sem("router_ex")
        router_done = sem("router_done")
        w_tr = sem("w_tr")
        wT_ready = sem("wT_ready")
        bias_mm = sem("bias_mm")
        bias_used = sem("bias_used")
        up_mm = sem("up_mm")
        gelu_done = sem("gelu_done")
        down_mm = sem("down_mm")
        down_used = sem("down_used")
        gate_ready = sem("gate_ready")
        xg_ready = sem("xg_ready")
        ring_cleared = sem("ring_cleared")
        kq_in = [sem(f"kq_in{i}") for i in range(2)]
        v_ready = sem("v_ready")
        scores_done = sem("scores_done")
        exp_done = sem("exp_done")
        pv_done = sem("pv_done")
        o_copied = sem("o_copied")
        o_tr = sem("o_tr")
        attn_ready = sem("attn_ready")
        attn_tr = sem("attn_tr")
        attnT_ready = sem("attnT_ready")
        proj_done = sem("proj_done")
        y_ready = sem("y_ready")
        y_stored = sem("y_stored")
        y_free = sem("y_free")
        exact_in = sem("exact_in")
        exact_mm = sem("exact_mm")
        exact_max = sem("exact_max")
        exact_max2 = sem("exact_max2")
        exact_tr = sem("exact_tr")
        exact_neg = sem("exact_neg")
        exact_hi = sem("exact_hi")
        exact_split = sem("exact_split")
        pe_gate = sem("pe_gate")
        dve_gate = sem("dve_gate")
        pool_gate = sem("pool_gate")
        act_dummy_ready = sem("act_dummy_ready")

        x_v = x.rearrange("b s d -> (b s) d").rearrange("(t p) d -> p t d", p=P)
        out_rows = out.rearrange("b s d -> (b s) d")

        def chained(eng, semaphore):
            count = [0]

            def link(ins):
                count[0] += 1
                ins.then_inc(semaphore, 1)
                eng.wait_ge(semaphore, count[0])
            return link, count

        block = ctx.enter_context(nc.Block())

        @block.sync
        def _(sp):
            for c in range(NT // XC):
                sp.dma_start(x_tok[:, c * XC:(c + 1) * XC, :], x_v[:, c * XC:(c + 1) * XC, :]).then_inc(x_in[c], 16)
            R = E * FC
            sp.dma_start(rows[0:R, :], b1.rearrange("e (c f) -> (e c) f", c=FC)).then_inc(rows_in, 16)
            sp.dma_start(rows[R:R + 1, :], ln_g.rearrange("(a d) -> a d", a=1)).then_inc(rows_in, 16)
            sp.dma_start(rows[R + 1:R + 2, :], ln_b.rearrange("(a d) -> a d", a=1)).then_inc(rows_in, 16)
            sp.dma_start(rows[R + 2:R + 3, :], bv.rearrange("(a d) -> a d", a=1)).then_inc(rows_in, 16)
            sp.dma_start(wv_sb[:, :], Wv).then_inc(rows_in, 16)
            sp.dma_start(wo_sb[:, :], Wo).then_inc(rows_in, 16)
            sp.dma_start(rw_sb[:, :], rW).then_inc(small_in, 16)
            sp.dma_start(bv_bc[:, :], bv.rearrange("(a d) -> a d", a=1).broadcast_to([P, D])).then_inc(small_in, 16)
            sp.dma_start(bo_bc[:, :], bo.rearrange("(a d) -> a d", a=1).broadcast_to([P, D])).then_inc(small_in, 16)
            sp.dma_start(rb_bc[:, :], rb.rearrange("(a d) -> a d", a=1).broadcast_to([P, E])).then_inc(small_in, 16)
            sp.dma_start(b2_sb[:, :], b2).then_inc(small_in, 16)
            sp.dma_start(w1_sb[:, :, :], W1.rearrange("e h f -> h e f")).then_inc(w1_in, 16)
            for e in range(E):
                sp.dma_start(w2_sb[:, e, :, :], W2[e].rearrange("(c p) h -> p c h", p=P)).then_inc(w2_in, 16)
            def store_parts(g, slot):
                sp.wait_ge(parts_ready, g + 1 + CREDIT)
                for blk in range(CIRC):
                    sp.dma_start(p_dram[:, blk, :, bass.ds(g * BLK, BLK)],
                                 parts[:, slot, blk % PARTS, :]).then_inc(parts_stored, 16)
                sp.wait_ge(m_ready, g + 1)
                sp.dma_start(m_dram[:, :, bass.ds(g * BLK, BLK)].rearrange("a h n -> h a n"), m_blk).then_inc(parts_stored, 16)
                sp.wait_ge(parts_stored, (g + 1) * 16 * (CIRC + 1))
                sp.sem_inc(parts_free, 1)

            with sp.Fori(0, NB // 2) as w:
                for i in range(2):
                    store_parts(w * 2 + i, i)
            sp.wait_ge(ring_cleared, 1)

            def load_heads(w, i, slot, loaded):
                for j in range(4):
                    head = p_dram[bass.ds((w % 2) * 8 + (4 * i + j), 1), :, :, bass.ds((w // 2) * S, S)].rearrange(
                        "h a d n -> (h a d) n")
                    sp.dma_start(k_ring[0:PROWS, slot, j, :],
                                 head[0:PARTS * DK, :].unsqueeze(0).broadcast_to([PARTS, PARTS * DK, S])).then_inc(loaded, 16)
                    for c in range(PARTS):
                        sp.dma_start(q_ring[c * PARTS * DK:(c + 1) * PARTS * DK, slot, j, :],
                                     head[c * DK:(c + PARTS) * DK, :]).then_inc(loaded, 16)

            sp.wait_ge(m2_ready, 1)
            m2_bits = sp.value_load(m2[0:1, 0:1].bitcast(I32))
            with sp.If(m2_bits > M2_LIMIT_BITS):
                with sp.Fori(0, NU // 2) as w:
                    for i in range(2):
                        sp.wait_ge(exact_mm, (w * 2 + i) * US * 2 + 1)
                        load_heads(w, i, 0, exact_in)
                sp.wait_ge(exact_mm, NU * US * 2 + 1)
                sp.wait_ge(exact_split, 1)
                sp.dma_start(m_dram[:, :, :].rearrange("a h n -> h a n"), m_parts).then_inc(m_stored, 16)
                sp.wait_ge(m_stored, 16)

            with sp.Fori(0, NU // 2) as w:
                for i in range(2):
                    sp.wait_ge(pv_done, (w * 2 + i - 1) * US + PV_CREDIT)
                    load_heads(w, i, i, kq_in[i])
                    sp.dma_start(q_ring[MROW:KROWS, i, :, :],
                                 m_dram[:, bass.ds((w % 2) * 8 + 4 * i, 4), bass.ds((w // 2) * S, S)]).then_inc(kq_in[i], 16)

        @block.gpsimd
        def _(pool):
            link, count = chained(pool, pool_chain)
            pool.memset(ident[:, :], 0.0).then_inc(pool_chain, 1)
            pool.memset(head_sel[:, :], 1.0).then_inc(pool_chain, 1)
            pool.memset(before[:, :, :], 1.0).then_inc(pool_chain, 1)
            count[0] += 3
            pool.wait_ge(pool_chain, count[0])
            pool.affine_select(out=ident[:, :], in_=ident[:, :], compare_op=ALU.not_equal, fill=1.0, base=0,
                               pattern=[[-1, P]], channel_multiplier=1).then_inc(consts_ready, 1)
            link(pool.affine_select(out=head_sel[:, :], in_=head_sel[:, :], compare_op=ALU.is_ge, fill=0.0, base=0,
                                    pattern=[[-DK, H]], channel_multiplier=1))
            pool.affine_select(out=head_sel[:, :], in_=head_sel[:, :], compare_op=ALU.is_ge, fill=0.0, base=DK - 1,
                               pattern=[[DK, H]], channel_multiplier=-1).then_inc(consts_ready, 1)
            pool.affine_select(out=before[:, :, :], in_=before[:, :, :], compare_op=ALU.is_gt, fill=0.0, base=0,
                               pattern=[[1, E], [-1, E]], channel_multiplier=0).then_inc(consts_ready, 1)
            pool.memset(ones[:, :], 1.0).then_inc(consts_ready, 1)
            pool.memset(v_tok[:, :, H * VW:VPAD], 0.0)
            v_heads = v_tok[:, :, 0:H * VW].rearrange("p t (h v) -> p t h v", v=VW)
            link(pool.memset(v_heads[:, :, :, DK], 1.0))
            pool.memset(q_ring[:, :, :, :].rearrange("p a b n -> p (a b n)").bitcast(U32), 0)
            link(pool.memset(k_ring[:, :, :, :].rearrange("p a b n -> p (a b n)").bitcast(U32), 0))
            pool.memset(k_ring[MROW:KROWS, :, :, :], 1.0).then_inc(ring_cleared, 1)
            pool.wait_ge(ring_cleared, 1)

            base = count[0]

            def split(w, i):
                g = w * 2 + i
                step = [0]

                def link_loop(ins):
                    step[0] += 1
                    ins.then_inc(pool_chain, 1)
                    pool.wait_ge(pool_chain, g * 4 + base + step[0])
                    pool.sem_inc(pool_gate, 1)

                pool.wait_ge(pT_copied, g + 1)
                pool.wait_ge(parts_free, g - 1 + CREDIT)
                pool.sem_inc(pool_gate, 1)
                src = pT[:, i, :]
                link_loop(pool.tensor_copy(parts[:, i, 0, :], src))
                link_loop(pool.tensor_tensor(src, src, parts[:, i, 0, :], ALU.subtract))
                link_loop(pool.tensor_copy(parts[:, i, 1, :], src))
                pool.tensor_tensor(parts[:, i, 2, :], src, parts[:, i, 1, :], ALU.subtract).then_inc(parts_ready, 1)
                pool.wait_ge(n2_copied, g + 1)
                pool.wait_ge(parts_free, g + CREDIT)
                pool.sem_inc(pool_gate, 1)
                link_loop(pool.tensor_copy(m_blk[:, 0, :], m_half))
                pool.tensor_tensor(m_blk[:, 1, :], m_half, m_blk[:, 0, :], ALU.subtract).then_inc(m_ready, 1)

            with pool.Fori(0, NB // 2) as w:
                for i in range(2):
                    split(w, i)

            def load_values(w, i):
                pool.tensor_copy(v_ring[:, i, :, :],
                                 v_tok[:, bass.ds((w // 2) * KT, KT), bass.ds((w % 2) * (8 * VW) + 4 * VW * i, VSLOT)]
                                 ).then_inc(v_ready, 1)

            def store(w, i):
                pool.wait_ge(y_ready, w * 2 + i + 2)
                pool.dma_start(out_rows[bass.ds((w * 2 + i) * UT * P, UT * P), :].rearrange("(t p) d -> p t d", p=P),
                               y_sb[:, :, :]).then_inc(y_stored, 16)
                pool.wait_ge(y_stored, (w * 2 + i + 1) * 16)
                pool.sem_inc(y_free, 1)

            pool.wait_ge(p_added, NB)
            pool.wait_ge(down_mm, NB * E + CREDIT)
            def step(w, first):
                for i in range(2):
                    pool.wait_ge(pv_done, (w * 2 + i - 1) * US + PV_CREDIT)
                    load_values(w, i)
                    if i == 1:
                        store(w, 0)
                    elif not first:
                        store(w - 1, 1)

            step(0, True)
            with pool.Fori(1, NU // 2) as w:
                step(w, False)
            store(NU // 2 - 1, 1)

        @block.scalar
        def _(act):
            act.wait_ge(wt_tr, 1)
            nc.scalar.copy(wvT[:, :], bank_m[0][:, 0:D])
            nc.scalar.copy(woT[:, :], bank_m[0][:, D:2 * D])
            nc.scalar.copy(cols[:, :], bank_m[0][:, 2 * D:2 * D + E * FC + 3]).then_inc(wt_copied, 1)
            act.wait_ge(wt_copied, 1)
            bv_col = cols[:, E * FC + 2:E * FC + 3]

            def prepare(g, slot, step, first=False):
                if step == 2:
                    act.wait_ge(xT_tr, g + 1)
                    if not first:
                        act.wait_ge(p_mm, g)
                    nc.scalar.copy(xnT, bank_m[0][:, :]).then_inc(xT_copied, 1)
                elif step == 3:
                    act.wait_ge(pT_mm, g + 1)
                    if not first:
                        act.wait_ge(n2_mm, g)
                    nc.scalar.activation(sqT, bank_m[0][:, :], ACT.Square, bias=bv_col).then_inc(sq_ready, 1)
                    act.wait_ge(parts_ready, g - 1 + CREDIT)
                    nc.scalar.activation(pT[:, slot, :], bank_m[0][:, :], ACT.Identity, bias=bv_col).then_inc(pT_copied, 1)
                elif step == 5:
                    act.wait_ge(router_d, g + 1)
                    nc.scalar.activation(ex[:, :, :], lg[:, :, :], ACT.Exp).then_inc(router_ex, 1)
                elif step == 6:
                    act.wait_ge(n2_mm, g + 1)
                    nc.scalar.copy(n2T[:, bass.ds(g * BLK, BLK)], bank_m[1][0:H, :])
                    if not first:
                        act.wait_ge(m_ready, g)
                    nc.scalar.activation(m_half, bank_m[1][0:H, :], ACT.Copy, scale=-0.5).then_inc(n2_copied, 1)

            def experts(u, i, last=False):
                for e in range(E):
                    for c in range(FC):
                        act.wait_ge(up_mm, (u * E + e) * FC + c + 1)
                        act.wait_ge(down_mm, u * E + e - 1 + CREDIT)
                        nc.scalar.activation(hid[:, e % 2, c, :], pair[e % 2][:, c, :], ACT.Gelu,
                                             bias=cols[:, e * FC + c:e * FC + c + 1]).then_inc(gelu_done, 1)
                    if e == 0:
                        act.wait_ge(w_tr, u + 1)
                        nc.scalar.copy(wT[:, :], bank_m[0][0:E, :]).then_inc(wT_ready, 1)
                    if not last:
                        prepare(u + 1, 1 - i, e)

            for step in range(E):
                prepare(0, 0, step, True)
            nc.scalar.activation(act_dummy[:, :], ones[:, 0:1], ACT.Gelu).then_inc(act_dummy_ready, 1)
            with act.Fori(0, NB // 2 - 1) as w:
                for i in range(2):
                    experts(w * 2 + i, i)
            experts(NB - 2, 0)
            experts(NB - 1, 1, last=True)
            act.wait_ge(down_used, NB * E + CREDIT)
            for c in range(4):
                part = xn_tok[:, c * NT // 4:(c + 1) * NT // 4, :]
                nc.scalar.activation(part, part, ACT.Silu).then_inc(gate_ready, 1)
            act.wait_ge(act_dummy_ready, 1)
            nc.scalar.activation(act_dummy[:, :], act_dummy[:, :], ACT.Exp)
            with act.Fori(0, NU // 2) as w:
                for i in range(2):
                    for k in range(US):
                        for half in range(2):
                            act.wait_ge(scores_done, ((w * 2 + i) * US + k) * 2 + half + 1)
                            if half == 0:
                                act.wait_ge(pv_done, (w * 2 + i) * US + k + 1 - ES + PV_CREDIT)
                            nc.scalar.activation(exps[:, k % ES, 2 * half:2 * half + 2, :], pair[half][:, :, :], ACT.Exp,
                                                 scale=SCALE).then_inc(exp_done, 1)

        @block.vector
        def _(dve):
            NORM_LINKS = 2 * (5 + 3 * NEWTON)
            LINKS = NORM_LINKS + 12

            def tile(tensor, t):
                return tensor[:, bass.ds(t, 1), :].rearrange("p a d -> p (a d)")

            def prepare(g, slot, step):
                at = {4: NORM_LINKS, 6: NORM_LINKS + 1}.get(step, 0)

                def link_block(ins):
                    nonlocal at
                    at += 1
                    ins.then_inc(dve_chain, 1)
                    dve.wait_ge(dve_chain, g * LINKS + at)

                if step == 0:
                    for source, into, ready in ((lambda t: tile(x_tok, g * TB + t), xn_blk[:, slot], xn_ready),
                                                (lambda t: xn_blk[:, slot, t, :], z0_blk, z0_ready)):
                        for t in range(TB):
                            ins = nc.vector.bn_stats(stats[:, t, :], source(t))
                        link_block(ins)
                        dve.sem_inc(dve_gate, 1)
                        for t in range(TB):
                            ins = nc.vector.bn_aggr(mv[:, t, :], stats[:, t, :])
                        link_block(ins)
                        link_block(nc.vector.tensor_scalar(veps[:, :], mv[:, :, 1], EPS, None, ALU.add))
                        link_block(nc.vector.tensor_scalar(rstd[:, :].bitcast(I32), veps[:, :].bitcast(I32), 1, None,
                                                           ALU.logical_shift_right))
                        link_block(nc.vector.tensor_scalar(rstd[:, :].bitcast(I32), rstd[:, :].bitcast(I32), -1, RSQRT_SEED,
                                                           ALU.mult, ALU.add))
                        for _ in range(NEWTON):
                            link_block(nc.vector.scalar_tensor_tensor(out=newton[:, :], in0=rstd[:, :], scalar=-0.5,
                                                                      in1=rstd[:, :], op0=ALU.mult, op1=ALU.mult))
                            link_block(nc.vector.tensor_tensor(newton[:, :], newton[:, :], veps[:, :], ALU.mult))
                            link_block(nc.vector.scalar_tensor_tensor(out=rstd[:, :], in0=newton[:, :], scalar=1.5,
                                                                      in1=rstd[:, :], op0=ALU.add, op1=ALU.mult))
                        for t in range(TB):
                            ins = nc.vector.tensor_scalar(into[:, t, :], source(t), mv[:, t, 0:1], rstd[:, t:t + 1],
                                                          ALU.subtract, ALU.mult)
                        ins.then_inc(ready, 1)
                        dve.wait_ge(ready, g + 1)
                elif step == 3:
                    dve.wait_ge(zT_tr, g + 1)
                    nc.vector.tensor_scalar(zT[:, slot, :], bank_m[1][:, :], g_col, b_col, ALU.mult, ALU.add).then_inc(zT_ready, 1)
                elif step == 4:
                    dve.wait_ge(logits_mm, g + 1)
                    nc.vector.tensor_tensor(lg[:, :, :], bank_m[1][:, 0:TB * E].rearrange("p (t e) -> p t e", e=E),
                                            rb_bc[:, :].unsqueeze(1).broadcast_to([P, TB, E]), ALU.add).then_inc(logits_used, 1)
                    dve.wait_ge(logits_used, g + 1)
                    link_block(nc.vector.tensor_reduce(red[:, :], lg[:, :, :], X, ALU.max))
                    nc.vector.tensor_tensor(lg[:, :, :], lg[:, :, :], red[:, :].unsqueeze(2).broadcast_to([P, TB, E]),
                                            ALU.subtract).then_inc(router_d, 1)
                elif step == 5:
                    dve.wait_ge(p_mm, g + 1)
                    v_heads = v_tok[:, bass.ds(g * TB, TB), 0:H * VW].rearrange("p t (h v) -> p t h v", v=VW)
                    nc.vector.tensor_tensor(v_heads[:, :, :, 0:DK], bank_m[0][:, :].rearrange("p (t h d) -> p t h d", h=H, d=DK),
                                            bv_bc[:, :].rearrange("p (h d) -> p h d", d=DK).unsqueeze(1).broadcast_to(
                                                [P, TB, H, DK]), ALU.add).then_inc(p_added, 1)
                elif step == 6:
                    dve.wait_ge(router_d, g + 1)
                    other = lg[:, :, :].unsqueeze(2).broadcast_to([P, TB, E, E])
                    own = lg[:, :, :].unsqueeze(3).broadcast_to([P, TB, E, E])
                    nc.vector.tensor_tensor(cmp_gt[:, :, :, :], other, own, ALU.is_gt)
                    link_block(nc.vector.tensor_tensor(cmp_eq[:, :, :, :], other, own, ALU.is_equal))
                    link_block(nc.vector.tensor_tensor(cmp_eq[:, :, :, :], cmp_eq[:, :, :, :],
                                                       before[:, :, :].unsqueeze(1).broadcast_to([P, TB, E, E]), ALU.mult))
                    link_block(nc.vector.tensor_tensor(cmp_gt[:, :, :, :], cmp_gt[:, :, :, :], cmp_eq[:, :, :, :], ALU.add))
                    link_block(nc.vector.tensor_reduce(rank[:, :, :], cmp_gt[:, :, :, :], X, ALU.add))
                    dve.wait_ge(router_ex, g + 1)
                    link_block(nc.vector.tensor_reduce(red[:, :], ex[:, :, :], X, ALU.add))
                    link_block(nc.vector.reciprocal(red2[:, :], red[:, :]))
                    link_block(nc.vector.tensor_tensor(ex[:, :, :], ex[:, :, :],
                                                       red2[:, :].unsqueeze(2).broadcast_to([P, TB, E]), ALU.mult))
                    link_block(nc.vector.scalar_tensor_tensor(out=ex[:, :, :], in0=rank[:, :, :], scalar=1.5, in1=ex[:, :, :],
                                                              op0=ALU.is_lt, op1=ALU.mult))
                    link_block(nc.vector.tensor_reduce(red[:, :], ex[:, :, :], X, ALU.add))
                    link_block(nc.vector.tensor_scalar(red[:, :], red[:, :], 1e-8, None, ALU.max))
                    link_block(nc.vector.reciprocal(red2[:, :], red[:, :]))
                    nc.vector.tensor_tensor(w_blk[:, slot, :, :], ex[:, :, :], red2[:, :].unsqueeze(2).broadcast_to([P, TB, E]),
                                            ALU.mult).then_inc(router_done, 1)
                    assert at == LINKS


            def largest_by_head():
                dve.wait_ge(n2_copied, NB)
                nc.vector.tensor_reduce(max_head[:, :], n2T, X, ALU.max).then_inc(max_head_ready, 1)

            def largest():
                dve.wait_ge(max_head_tr, 1)
                nc.vector.tensor_reduce(m2[:, :], bank_m[0][0:1, 0:H], X, ALU.max).then_inc(m2_ready, 1)

            def experts(u, i, last=False):
                if last:
                    largest_by_head()
                else:
                    prepare(u + 1, 1 - i, 0)
                dve.wait_ge(down_used, u * E + CREDIT)
                dve.wait_ge(bias_mm, u + 1)
                nc.vector.tensor_tensor(acc[:, :, :], bank_m[1][:, :].rearrange("p (t d) -> p t d", t=TB),
                                        xn_blk[:, i, :, :], ALU.add).then_inc(bias_used, 1)
                dve.wait_ge(router_done, u + 1)
                for e in range(E):
                    dve.wait_ge(down_mm, u * E + e + 1 + CREDIT)
                    if e == 0:
                        dve.wait_ge(bias_used, u + 1)
                    else:
                        dve.wait_ge(down_used, u * E + e + CREDIT)
                    for t in range(TB):
                        into = acc[:, t, :] if e < E - 1 else tile(xn_tok, u * TB + t)
                        ins = nc.vector.scalar_tensor_tensor(
                            out=into, in0=bank_o[e % 2][:, t * D:(t + 1) * D],
                            scalar=w_blk[:, i, t, e:e + 1], in1=acc[:, t, :], op0=ALU.mult, op1=ALU.add)
                    ins.then_inc(down_used, 1)
                    if not last and e + 2 < E:
                        prepare(u + 1, 1 - i, e + 2)
                    if last and e == 0:
                        largest()

            dve.wait_ge(x_in[0], 16)
            prepare(0, 0, 0)
            dve.wait_ge(wt_copied, 1)
            dve.wait_ge(small_in, 16 * 5)
            dve.wait_ge(consts_ready, 4)
            g_col = cols[:, E * FC:E * FC + 1]
            b_col = cols[:, E * FC + 1:E * FC + 2]
            for step in range(1, E):
                prepare(0, 0, step)
            for c in range(1, NT // XC):
                dve.wait_ge(x_in[c], 16)
            with dve.Fori(0, NB // 2 - 1) as w:
                for i in range(2):
                    experts(w * 2 + i, i)
            experts(NB - 2, 0)
            experts(NB - 1, 1, last=True)
            link2_base = LINKS * NB
            for c in range(4):
                gate = xn_tok[:, c * NT // 4:(c + 1) * NT // 4, :]
                into = x_tok[:, c * NT // 4:(c + 1) * NT // 4, :]
                tmp = scratch[:, c * N // 4:(c + 1) * N // 4].rearrange("p (t d) -> p t d", d=D)
                dve.wait_ge(gate_ready, c + 1)
                nc.vector.tensor_tensor(tmp, gate, bo_bc[:, :].unsqueeze(1).broadcast_to([P, NT // 4, D]),
                                        ALU.mult).then_inc(dve_chain, 1)
                dve.wait_ge(dve_chain, link2_base + 2 * c + 1)
                nc.vector.tensor_tensor(into, into, tmp, ALU.add).then_inc(dve_chain, 1)
                dve.wait_ge(dve_chain, link2_base + 2 * c + 2)
            base2 = link2_base + 8
            m2_bits = dve.value_load(m2[0:1, 0:1].bitcast(I32))
            with dve.If(m2_bits > M2_LIMIT_BITS):
                with dve.Fori(0, NU // 2) as w:
                    for i in range(2):
                        for k in range(US):
                            qh, kt = divmod(k, KT)
                            for half in range(2):
                                step = ((w * 2 + i) * US + k) * 2 + half
                                dve.wait_ge(exact_mm, step + 2)
                                into = row_max[:, bass.ds((w // 2) * KT + kt, 1), bass.ds((w % 2) * 8 + (4 * i + 2 * half), 2), qh]
                                nc.vector.tensor_reduce(into.rearrange("p t h -> p (t h)"), pair[half][:, :, :], X,
                                                        ALU.max).then_inc(exact_max, 1)
                dve.wait_ge(exact_max, NU * US * 2 + CREDIT)
                nc.vector.tensor_reduce(row_max2, row_max, X, ALU.max).then_inc(exact_max2, 1)
                dve.wait_ge(m_ready, NB)
                for g in range(NB):
                    dve.wait_ge(exact_tr, g + 1)
                    nc.vector.tensor_scalar(n2T[:, g * BLK:(g + 1) * BLK], bank_m[g % 2][0:H, :], -1.0, None,
                                            ALU.mult).then_inc(exact_neg, 1)
                dve.wait_ge(exact_neg, NB)
                nc.vector.tensor_copy(m_parts[:, 0, :], n2T).then_inc(exact_hi, 1)
                dve.wait_ge(exact_hi, 1)
                nc.vector.tensor_tensor(m_parts[:, 1, :], n2T, m_parts[:, 0, :], ALU.subtract).then_inc(exact_split, 1)
            per_unit = QR // 4 + 1
            with dve.Fori(0, NU // 2) as w:
                for i in range(2):
                    n = w * 2 + i
                    for qh in range(QH):
                        dve.wait_ge(pv_done, n * US + (qh + 1) * KT + PV_CREDIT)
                        nc.vector.tensor_copy(o_sb[:, qh * BLK:(qh + 1) * BLK], bank_o[qh][:, :]).then_inc(o_copied, 1)
                    for r in range(QR // 4):
                        dve.wait_ge(o_tr, n * (QR // 4) + r + 1)
                        o_rows = bank_m[r % 2][0:RH, :].rearrange("p (q j v) -> p q j v", q=4, j=4)
                        nc.vector.reciprocal(rden[:, r % 2, :, :], o_rows[:, :, :, DK]).then_inc(dve_chain, 1)
                        dve.wait_ge(dve_chain, n * per_unit + base2 + r + 1)
                        nc.vector.tensor_tensor(attn[:, :, 4 * r:4 * r + 4, :].rearrange("p j q d -> p q j d"),
                                                o_rows[:, :, :, 0:DK], rden[:, r % 2, :, :].unsqueeze(3).broadcast_to([RH, 4, 4, DK]),
                                                ALU.mult).then_inc(attn_ready, 1)
                    dve.wait_ge(attn_tr, n + 1)
                    nc.vector.tensor_copy(attnT[:, :], bank_m[0][:, 0:4 * RH]).then_inc(attnT_ready, 1)
                    dve.wait_ge(proj_done, n + 1)
                    dve.wait_ge(y_free, n + 1)
                    nc.vector.tensor_tensor(y_sb[:, :, :], bank_m[1][:, 0:UT * D].rearrange("p (t d) -> p t d", t=UT),
                                            xn_tok[:, bass.ds(n * UT, UT), :], ALU.mult).then_inc(dve_chain, 1)
                    dve.wait_ge(dve_chain, n * per_unit + base2 + per_unit)
                    nc.vector.tensor_tensor(y_sb[:, :, :], y_sb[:, :, :], x_tok[:, bass.ds(n * UT, UT), :],
                                            ALU.add).then_inc(y_ready, 1)

        @block.tensor
        def _(pe):
            pe.sem_inc(parts_ready, CREDIT)
            pe.sem_inc(parts_free, CREDIT)
            pe.sem_inc(down_mm, CREDIT)
            pe.sem_inc(down_used, CREDIT)
            pe.sem_inc(exp_done, CREDIT)
            pe.sem_inc(o_copied, CREDIT)
            pe.sem_inc(y_ready, 1)
            pe.sem_inc(y_free, 1)
            pe.sem_inc(exact_mm, 1)
            pe.sem_inc(exact_max, CREDIT)
            pe.sem_inc(pv_done, PV_CREDIT)
            pe.wait_ge(consts_ready, 4)
            pe.wait_ge(rows_in, 16 * 6)
            nc.tensor.transpose(bank_m[0][:, 0:D], wv_sb[:, :], ident[:, :])
            nc.tensor.transpose(bank_m[0][:, D:2 * D], wo_sb[:, :], ident[:, :])
            R = E * FC + 3
            nc.tensor.transpose(bank_m[0][:, 2 * D:2 * D + R], rows[:, :], ident[0:R, 0:R]).then_inc(wt_tr, 1)
            pe.wait_ge(wt_copied, 1)
            pe.wait_ge(small_in, 16 * 5)

            def prepare(g, slot, step, first=False):
                if step == 2:
                    pe.wait_ge(xn_ready, g + 1)
                    for t in range(TB):
                        ins = nc.tensor.transpose(bank_m[0][:, t * P:(t + 1) * P], xn_blk[:, slot, t, :], ident[:, :])
                    ins.then_inc(xT_tr, 1)
                elif step == 3:
                    pe.wait_ge(z0_ready, g + 1)
                    if not first:
                        pe.wait_ge(bias_used, g)
                    for t in range(TB):
                        ins = nc.tensor.transpose(bank_m[1][:, t * P:(t + 1) * P], z0_blk[:, t, :], ident[:, :])
                    ins.then_inc(zT_tr, 1)
                    pe.wait_ge(xT_copied, g + 1)
                    nc.tensor.matmul(bank_m[0][:, :], wvT[:, :], xnT, start=True, stop=True).then_inc(pT_mm, 1)
                elif step == 4:
                    pe.wait_ge(zT_ready, g + 1)
                    for t in range(TB):
                        ins = nc.tensor.matmul(bank_m[1][:, t * E:(t + 1) * E], zT[:, slot, t * P:(t + 1) * P], rw_sb[:, :],
                                               start=True, stop=True)
                    ins.then_inc(logits_mm, 1)
                elif step == 5:
                    pe.wait_ge(sq_ready, g + 1)
                    pe.wait_ge(pT_copied, g + 1)
                    for t in range(TB):
                        ins = nc.tensor.matmul(bank_m[0][:, t * D:(t + 1) * D], xnT[:, t * P:(t + 1) * P], wvT[:, :],
                                               start=True, stop=True)
                    ins.then_inc(p_mm, 1)
                elif step == 6:
                    pe.wait_ge(logits_used, g + 1)
                    nc.tensor.matmul(bank_m[1][0:H, :], head_sel[:, :], sqT, start=True, stop=True).then_inc(n2_mm, 1)

            def experts(u, i, last=False):
                def up(e):
                    for c in range(FC):
                        nc.tensor.matmul(pair[e % 2][:, c, :], w1_sb[:, e, c * P:(c + 1) * P], zT[:, i, :],
                                         start=True, stop=True).then_inc(up_mm, 1)

                def down(e):
                    pe.wait_ge(gelu_done, (u * E + e + 1) * FC)
                    pe.wait_ge(down_used, u * E + e - 1 + CREDIT)
                    for t in range(TB):
                        for c in range(FC):
                            ins = nc.tensor.matmul(bank_o[e % 2][:, t * D:(t + 1) * D], hid[:, e % 2, c, t * P:(t + 1) * P],
                                                   w2_sb[:, e, c, :], start=(c == 0), stop=(c == FC - 1))
                    ins.then_inc(down_mm, 1)

                for e in range(E):
                    if e >= 2:
                        down(e - 2)
                    up(e)
                    if e == 0:
                        pe.wait_ge(router_done, u + 1)
                        pe.wait_ge(p_added, u + 1)
                        for t in range(TB):
                            ins = nc.tensor.transpose(bank_m[0][0:E, t * P:(t + 1) * P], w_blk[:, i, t, :], ident[:, :])
                        ins.then_inc(w_tr, 1)
                    elif e == 1:
                        pe.wait_ge(wT_ready, u + 1)
                        pe.wait_ge(n2_copied, u + 1)
                        for t in range(TB):
                            ins = nc.tensor.matmul(bank_m[1][:, t * D:(t + 1) * D], wT[:, t * P:(t + 1) * P], b2_sb[:, :],
                                                   start=True, stop=True)
                        ins.then_inc(bias_mm, 1)
                    elif not last:
                        prepare(u + 1, 1 - i, e)
                    elif e == 2:
                        pe.wait_ge(max_head_ready, 1)
                        nc.tensor.transpose(bank_m[0][0:1, 0:H], max_head[:, :], ident[0:H, 0:H]).then_inc(max_head_tr, 1)
                down(E - 2)
                down(E - 1)

            for step in range(E):
                prepare(0, 0, step, True)
            pe.wait_ge(zT_ready, 1)
            pe.wait_ge(w1_in, 16)
            pe.wait_ge(w2_in, 16 * E)
            with pe.Fori(0, NB // 2 - 1) as w:
                for i in range(2):
                    experts(w * 2 + i, i)
            experts(NB - 2, 0)
            experts(NB - 1, 1, last=True)
            pe.wait_ge(down_used, NB * E + CREDIT)
            pe.wait_ge(m2_ready, 1)
            m2_bits = pe.value_load(m2[0:1, 0:1].bitcast(I32))
            with pe.If(m2_bits > M2_LIMIT_BITS):
                with pe.Fori(0, NU // 2) as w:
                    for i in range(2):
                        pe.wait_ge(exact_in, (w * 2 + i + 1) * 16 * (KQ_LOADS - 1))
                        for k in range(US):
                            qh, kt = divmod(k, KT)
                            for half in range(2):
                                step = ((w * 2 + i) * US + k) * 2 + half
                                pe.wait_ge(exact_max, step - 1 + CREDIT)
                                for j in range(2 * half, 2 * half + 2):
                                    ins = nc.tensor.matmul(pair[half][:, j % 2, :], k_ring[0:PROWS, 0, j, kt * P:(kt + 1) * P],
                                                           q_ring[0:PROWS, 0, j, qh * BLK:(qh + 1) * BLK], start=True, stop=True)
                                ins.then_inc(exact_mm, 1)
                pe.wait_ge(exact_max2, 1)
                for g in range(NB):
                    if g >= 2:
                        pe.wait_ge(exact_neg, g - 1)
                    for t in range(TB):
                        ins = nc.tensor.transpose(bank_m[g % 2][0:H, t * P:(t + 1) * P], row_max2[:, g * TB + t, :], ident[:, :])
                    ins.then_inc(exact_tr, 1)
                pe.wait_ge(exact_split, 1)

            def scores(w, i, k, half):
                qh, kt = divmod(k, KT)
                n = w * 2 + i
                if k == 0 and half == 0:
                    pe.wait_ge(kq_in[i], (w + 1) * 16 * KQ_LOADS)
                pe.wait_ge(exp_done, (n * US + k) * 2 + half - 1 + CREDIT)
                for j in range(2 * half, 2 * half + 2):
                    ins = nc.tensor.matmul(pair[half][:, j % 2, :], k_ring[0:KROWS, i, j, kt * P:(kt + 1) * P],
                                           q_ring[0:KROWS, i, j, qh * BLK:(qh + 1) * BLK], start=True, stop=True)
                ins.then_inc(scores_done, 1)

            def values(w, i, k):
                qh, kt = divmod(k, KT)
                n = w * 2 + i
                pe.wait_ge(exp_done, (n * US + k + 1) * 2 + CREDIT)
                if k == 0:
                    pe.wait_ge(v_ready, n + 1)
                if kt == 0:
                    pe.wait_ge(o_copied, n * 2 + qh - 1 + CREDIT)
                for j in range(4):
                    ins = nc.tensor.matmul(bank_o[qh][32 * j:32 * j + 32, :], v_ring[:, i, kt, VW * j:VW * j + 32],
                                           exps[:, k % ES, j, :], start=(kt == 0), stop=(kt == KT - 1))
                ins.then_inc(pv_done, 1)

            FINISH = QR // 4 + 2

            def finish(w, i, step):
                n = w * 2 + i
                if step < QR // 4:
                    if step == 0:
                        pe.wait_ge(o_copied, n * 2 + 2 + CREDIT)
                        pe.wait_ge(y_ready, n + 1)
                    if step >= 2:
                        pe.wait_ge(attn_ready, n * (QR // 4) + step - 1)
                    pe.sem_inc(pe_gate, 1)
                    queries = o_sb.rearrange("p (r s) -> p s r", s=QR)
                    for q in range(4):
                        ins = nc.tensor.transpose(bank_m[step % 2][0:RH, q * P:(q + 1) * P], queries[:, 4 * step + q, :],
                                                  ident[:, :])
                    ins.then_inc(o_tr, 1)
                elif step == QR // 4:
                    pe.wait_ge(attn_ready, (n + 1) * (QR // 4))
                    pe.sem_inc(pe_gate, 1)
                    for j in range(4):
                        ins = nc.tensor.transpose(bank_m[0][:, j * RH:(j + 1) * RH],
                                                  attn[:, j, :, :].rearrange("p q d -> p (q d)"), ident[0:RH, 0:RH])
                    ins.then_inc(attn_tr, 1)
                else:
                    pe.wait_ge(attnT_ready, n + 1)
                    for t in range(UT):
                        ins = nc.tensor.matmul(bank_m[1][:, t * D:(t + 1) * D], attnT[:, t * P:(t + 1) * P], woT[:, :],
                                               start=True, stop=True)
                    ins.then_inc(proj_done, 1)

            def two_units(w, first):
                for g in range(2 * US):
                    i, k = divmod(g, US)
                    scores(w, i, k, 0)
                    if g >= VLAG:
                        values(w, *divmod(g - VLAG, US))
                    elif not first:
                        values(w - 1, 1, US + g - VLAG)
                    scores(w, i, k, 1)
                    if k - VLAG in FINISH_AT:
                        step = FINISH_AT.index(k - VLAG)
                        if i == 1:
                            finish(w, 0, step)
                        elif not first:
                            finish(w - 1, 1, step)

            VLAG = 2
            FINISH_AT = [1, 2, 3, 4, 6, 8]
            assert len(FINISH_AT) == FINISH
            two_units(0, True)
            with pe.Fori(1, NU // 2) as w:
                two_units(w, False)
            for k in range(US - VLAG, US):
                values(NU // 2 - 1, 1, k)
            for step in range(FINISH):
                finish(NU // 2 - 1, 1, step)


_INS = ['L0_attn_x', 'L0_attn_Wv', 'L0_attn_bv', 'L0_attn_Wo', 'L0_attn_bo', 'L0_ffn_ln_g', 'L0_ffn_ln_b', 'L0_ffn_rW',
        'L0_ffn_rb', 'L0_ffn_W1', 'L0_ffn_b1', 'L0_ffn_W2', 'L0_ffn_b2']


def kernel(**inputs):
    import numpy as _np
    import concourse.bacc as _bacc
    from concourse.bass_utils import run_bass_kernel_spmd as _run

    nc = _bacc.Bacc("TRN2", target_bir_lowering=False, num_devices=1)
    arrays, args = {}, []
    for name in _INS:
        a = _np.ascontiguousarray(inputs[name])
        arrays[f"in_{name}"] = a
        args.append(nc.dram_tensor(f"in_{name}", a.shape, mybir.dt.from_np(a.dtype), kind="ExternalInput").ap())
    result = nc.dram_tensor("out_x", (B, S, D), F32, kind="ExternalOutput").ap()
    build(nc, *args, result)
    r = _run(nc, [arrays], core_ids=[0])
    return r.results[0]["out_x"]
```

```python
from contextlib import ExitStack

import concourse.bass as bass
import numpy as np
from concourse import mybir

F32 = mybir.dt.float32
F32R = mybir.dt.float32r
BF16 = mybir.dt.bfloat16
I32 = mybir.dt.int32
U32 = mybir.dt.uint32
ALU = mybir.AluOpType
ACT = mybir.ActivationFunctionType
X = mybir.AxisListType.X

P = 128
B, S, D = 4, 1024, 128
H = 16
DK = D // H
N = B * S
NT = N // P
BLK = 512
NB = N // BLK
TB = BLK // P
E = 8
HF = 256
FC = HF // P
EPS = 1e-5
HG = H // 4
KT = S // P
QH = S // BLK
NU = B * HG
US = QH * KT
QR = D // DK
RH = S // QR
UT = 4 * RH // P
HR = RH // QH
assert HR == 32
PARTS = 3
PROWS = PARTS * PARTS * DK
MROW = 96
MPARTS = 2
KROWS = MROW + MPARTS
VW = DK + 1
VPAD = H * VW + 32 - VW
VSLOT = 3 * VW + 32
SCALE = float(DK) ** -0.5
RSQRT_SEED = 0x5F3759DF
NEWTON = 3
M2_LIMIT = 400.0
M2_LIMIT_BITS = int(np.float32(M2_LIMIT).view(np.int32))
CREDIT = 2
PV_CREDIT = US + 1
ES = 4
PRODUCTS = ((0, 0), (0, 1), (1, 0))
KQ_LOADS = 4 * (1 + PARTS) + 1
XC = 8


def build(nc, x, Wv, bv, Wo, bo, ln_g, ln_b, rW, rb, W1, b1, W2, b2, out):
    ctx = ExitStack()
    with ctx:
        def sb(name, shape, dt=F32):
            return ctx.enter_context(nc.sbuf_tensor(name, shape, dt))

        def sem(name):
            return ctx.enter_context(nc.semaphore(name))

        x_tok = sb("x_tok", [P, NT, D])
        xn_tok = sb("xn_tok", [P, NT, D])
        local = sb("local", [P, 8, BLK])
        scratch = sb("scratch", [P, NT * H * (QH + 1)])
        pT = sb("pT", [P, 2, BLK])
        sqT = sb("sqT", [P, BLK], BF16)
        parts = sb("parts", [P, 2, PARTS, BLK], BF16)
        v_tok = sb("v_tok", [P, NT, VPAD])
        w2_sb = sb("w2_sb", [P, E, FC, D])
        hid = sb("hid", [P, 2, FC, BLK])
        exps = sb("exps", [P, ES, 4, BLK])
        k_ring = sb("k_ring", [P, 2, 4, S], BF16)
        q_ring = sb("q_ring", [P, 2, 4, S], BF16)
        acc = sb("acc", [P, TB, D])
        attn = sb("attn", [P, QH, QR, DK])
        attnT = sb("attnT", [P, 4 * RH])
        act_dummy = sb("act_dummy", [1, 1])
        y_sb = sb("y_sb", [P, UT, D])
        ident = sb("ident", [P, P])
        ones = sb("ones", [1, 1])
        head_sel = sb("head_sel", [P, H], BF16)
        before = sb("before", [P, E, E])
        wv_sb = sb("wv_sb", [P, D])
        wo_sb = sb("wo_sb", [P, D])
        wvT = sb("wvT", [P, D])
        woT = sb("woT", [P, D])
        rows = sb("rows", [E * FC + 3, P])
        cols = sb("cols", [P, E * FC + 3])
        bo_bc = sb("bo_bc", [P, D])
        rb_bc = sb("rb_bc", [P, E])
        rw_sb = sb("rw_sb", [P, E])
        b2_sb = sb("b2_sb", [E, D])
        stats = sb("stats", [P, TB, 6])
        mv = sb("mv", [P, TB, 2])
        veps = sb("veps", [P, TB])
        newton = sb("newton", [P, TB])
        rstd = sb("rstd", [P, TB])
        lg = sb("lg", [P, TB, E])
        ex = sb("ex", [P, TB, E])
        rank = sb("rank", [P, TB, E])
        red = sb("red", [P, TB])
        red2 = sb("red2", [P, TB])
        cmp_gt = sb("cmp_gt", [P, TB, E, E])
        cmp_eq = sb("cmp_eq", [P, TB, E, E])
        w_blk = sb("w_blk", [P, 2, TB, E])
        wT = sb("wT", [E, BLK])
        max_head = sb("max_head", [H, 1])
        m2 = sb("m2", [1, 1])
        rden = sb("rden", [P, QH, QR])
        xn_blk = local[:, 0:2, :].rearrange("p a (t d) -> p a t d", d=D)
        zT = local[:, 2:4, :]
        z0_blk = local[:, 4, :].rearrange("p (t d) -> p t d", d=D)
        xnT = local[:, 5, :]
        w1_parts = sb("w1_parts", [P, 2, E, HF], F32R)
        z_parts = sb("z_parts", [P, 2, 2, BLK], F32R)
        n2T = exps[0:H, 0:2, :, :].rearrange("p a b n -> p (a b n)")
        m_half = local[0:H, 6, :]
        m_blk = local[0:H, 7, :].bitcast(BF16).rearrange("p (a n) -> p a n", a=MPARTS)
        w1_sb = exps[:, 2, :, :].rearrange("p a n -> p (a n)").rearrange("p (e f) -> p e f", e=E)
        o_turned = scratch[:, 0:QH * QR * 32].rearrange("p (a q v) -> p a q v", a=QH, q=QR)
        v_ring = w2_sb[:, :, :, :].rearrange("p e c d -> p (e c d)")[:, 0:2 * KT * VSLOT].rearrange(
            "p (a k v) -> p a k v", a=2, k=KT)

        row_max = scratch[:, 0:NT * H * QH].rearrange("p (t h q) -> p t h q", h=H, q=QH)
        m_parts = exps[0:H, 2:4, :, :].rearrange("p a b n -> p (a b n)").bitcast(BF16).rearrange("p (a n) -> p a n", a=MPARTS)
        row_max2 = scratch[:, NT * H * QH:NT * H * (QH + 1)].rearrange("p (t h) -> p t h", h=H)

        pair = [ctx.enter_context(nc.psum_tensor(f"pair{i}", [P, 2, BLK], F32)) for i in range(3)]
        bank_o = [ctx.enter_context(nc.psum_tensor(f"bank_o{i}", [P, BLK], F32)) for i in range(2)]
        bank_m = [pair[2][:, i, :] for i in range(2)]
        bank_v, bank_f = bank_o

        CIRC = 2 * PARTS - 1
        p_dram = nc.dram_tensor("p_dram", [H, CIRC, DK, N], BF16)
        m_dram = nc.dram_tensor("m_dram", [MPARTS, H, N], BF16)

        x_in = [sem(f"x_in{c}") for c in range(NT // XC)]
        small_in = sem("small_in")
        rows_in = sem("rows_in")
        w1_in = sem("w1_in")
        w2_in = sem("w2_in")
        consts_ready = sem("consts_ready")
        pool_chain = sem("pool_chain")
        dve_chain = sem("dve_chain")
        xn_ready = sem("xn_ready")
        z0_ready = sem("z0_ready")
        wt_tr = sem("wt_tr")
        wt_copied = sem("wt_copied")
        xT_tr = sem("xT_tr")
        xT_copied = sem("xT_copied")
        zT_tr = sem("zT_tr")
        zT_ready = sem("zT_ready")
        z_hi = sem("z_hi")
        z_split = sem("z_split")
        w1_hi = sem("w1_hi")
        w1_split = sem("w1_split")
        logits_mm = sem("logits_mm")
        logits_used = sem("logits_used")
        p_tr = sem("p_tr")
        p_copied = sem("p_copied")
        pT_mm = sem("pT_mm")
        pT_copied = sem("pT_copied")
        sq_ready = sem("sq_ready")
        n2_mm = sem("n2_mm")
        n2_copied = sem("n2_copied")
        parts_ready = sem("parts_ready")
        parts_stored = sem("parts_stored")
        parts_free = sem("parts_free")
        max_head_ready = sem("max_head_ready")
        max_head_tr = sem("max_head_tr")
        m2_ready = sem("m2_ready")
        m_ready = sem("m_ready")
        m_stored = sem("m_stored")
        router_d = sem("router_d")
        router_ex = sem("router_ex")
        router_done = sem("router_done")
        w_tr = sem("w_tr")
        wT_ready = sem("wT_ready")
        bias_mm = sem("bias_mm")
        bias_used = sem("bias_used")
        up_mm = sem("up_mm")
        gelu_done = sem("gelu_done")
        down_mm = sem("down_mm")
        down_used = sem("down_used")
        gate_ready = sem("gate_ready")
        ring_cleared = sem("ring_cleared")
        kq_in = [sem(f"kq_in{i}") for i in range(2)]
        v_ready = sem("v_ready")
        scores_done = sem("scores_done")
        exp_done = sem("exp_done")
        pv_done = sem("pv_done")
        o_turned_ready = sem("o_turned_ready")
        attn_ready = sem("attn_ready")
        attn_tr = sem("attn_tr")
        attnT_ready = sem("attnT_ready")
        proj_done = sem("proj_done")
        y_ready = sem("y_ready")
        y_stored = sem("y_stored")
        y_free = sem("y_free")
        exact_in = sem("exact_in")
        exact_mm = sem("exact_mm")
        exact_max = sem("exact_max")
        exact_max2 = sem("exact_max2")
        exact_tr = sem("exact_tr")
        exact_neg = sem("exact_neg")
        exact_hi = sem("exact_hi")
        exact_split = sem("exact_split")
        dve_gate = sem("dve_gate")
        pool_gate = sem("pool_gate")
        act_dummy_ready = sem("act_dummy_ready")

        x_v = x.rearrange("b s d -> (b s) d").rearrange("(t p) d -> p t d", p=P)
        out_rows = out.rearrange("b s d -> (b s) d")

        def chained(eng, semaphore):
            count = [0]

            def link(ins):
                count[0] += 1
                ins.then_inc(semaphore, 1)
                eng.wait_ge(semaphore, count[0])
            return link, count

        block = ctx.enter_context(nc.Block())

        @block.sync
        def _(sp):
            def load_x(c):
                sp.dma_start(x_tok[:, c * XC:(c + 1) * XC, :], x_v[:, c * XC:(c + 1) * XC, :]).then_inc(x_in[c], 16)
            load_x(0)
            R = E * FC
            sp.dma_start(rows[0:R, :], b1.rearrange("e (c f) -> (e c) f", c=FC)).then_inc(rows_in, 16)
            sp.dma_start(rows[R:R + 1, :], ln_g.rearrange("(a d) -> a d", a=1)).then_inc(rows_in, 16)
            sp.dma_start(rows[R + 1:R + 2, :], ln_b.rearrange("(a d) -> a d", a=1)).then_inc(rows_in, 16)
            sp.dma_start(rows[R + 2:R + 3, :], bv.rearrange("(a d) -> a d", a=1)).then_inc(rows_in, 16)
            sp.dma_start(wv_sb[:, :], Wv).then_inc(rows_in, 16)
            sp.dma_start(wo_sb[:, :], Wo).then_inc(rows_in, 16)
            sp.dma_start(rw_sb[:, :], rW).then_inc(small_in, 16)
            sp.dma_start(bo_bc[:, :], bo.rearrange("(a d) -> a d", a=1).broadcast_to([P, D])).then_inc(small_in, 16)
            sp.dma_start(rb_bc[:, :], rb.rearrange("(a d) -> a d", a=1).broadcast_to([P, E])).then_inc(small_in, 16)
            sp.dma_start(b2_sb[:, :], b2).then_inc(small_in, 16)
            sp.dma_start(w1_sb[:, :, :], W1.rearrange("e h f -> h e f")).then_inc(w1_in, 16)
            for c in range(1, NT // XC):
                load_x(c)
            for e in range(E):
                sp.dma_start(w2_sb[:, e, :, :], W2[e].rearrange("(c p) h -> p c h", p=P)).then_inc(w2_in, 16)
            def store_parts(g, slot):
                sp.wait_ge(parts_ready, g + 1 + CREDIT)
                for blk in range(CIRC):
                    sp.dma_start(p_dram[:, blk, :, bass.ds(g * BLK, BLK)],
                                 parts[:, slot, blk % PARTS, :]).then_inc(parts_stored, 16)
                sp.wait_ge(m_ready, g + 1)
                sp.dma_start(m_dram[:, :, bass.ds(g * BLK, BLK)].rearrange("a h n -> h a n"), m_blk).then_inc(parts_stored, 16)
                sp.wait_ge(parts_stored, (g + 1) * 16 * (CIRC + 1))
                sp.sem_inc(parts_free, 1)

            with sp.Fori(0, NB // 2) as w:
                for i in range(2):
                    store_parts(w * 2 + i, i)
            sp.wait_ge(ring_cleared, 1)

            def load_heads(w, i, slot, loaded):
                for j in range(4):
                    head = p_dram[bass.ds((w % 2) * 8 + (4 * i + j), 1), :, :, bass.ds((w // 2) * S, S)].rearrange(
                        "h a d n -> (h a d) n")
                    sp.dma_start(k_ring[0:PROWS, slot, j, :],
                                 head[0:PARTS * DK, :].unsqueeze(0).broadcast_to([PARTS, PARTS * DK, S])).then_inc(loaded, 16)
                    for c in range(PARTS):
                        sp.dma_start(q_ring[c * PARTS * DK:(c + 1) * PARTS * DK, slot, j, :],
                                     head[c * DK:(c + PARTS) * DK, :]).then_inc(loaded, 16)

            load_heads(0, 0, 0, kq_in[0])
            sp.wait_ge(m2_ready, 1)
            m2_bits = sp.value_load(m2[0:1, 0:1].bitcast(I32))
            with sp.If(m2_bits > M2_LIMIT_BITS):
                sp.wait_ge(kq_in[0], 16 * (KQ_LOADS - 1))
                with sp.Fori(0, NU // 2) as w:
                    for i in range(2):
                        sp.wait_ge(exact_mm, (w * 2 + i) * US * 2 + 1)
                        load_heads(w, i, 0, exact_in)
                sp.wait_ge(exact_mm, NU * US * 2 + 1)
                sp.wait_ge(exact_split, 1)
                sp.dma_start(m_dram[:, :, :].rearrange("a h n -> h a n"), m_parts).then_inc(m_stored, 16)
                sp.wait_ge(m_stored, 16)
                load_heads(0, 0, 0, exact_in)
                sp.wait_ge(exact_in, (NU + 1) * 16 * (KQ_LOADS - 1))

            def load_stabiliser(w, i):
                sp.dma_start(q_ring[MROW:KROWS, i, :, :],
                             m_dram[:, bass.ds((w % 2) * 8 + 4 * i, 4), bass.ds((w // 2) * S, S)]).then_inc(kq_in[i], 16)

            def load_unit(w, i):
                sp.wait_ge(pv_done, (w * 2 + i - 1) * US + PV_CREDIT)
                load_heads(w, i, i, kq_in[i])
                load_stabiliser(w, i)

            load_stabiliser(0, 0)
            load_unit(0, 1)
            with sp.Fori(1, NU // 2) as w:
                for i in range(2):
                    load_unit(w, i)

        @block.gpsimd
        def _(pool):
            link, count = chained(pool, pool_chain)
            pool.memset(ident[:, :], 0.0).then_inc(pool_chain, 1)
            pool.memset(head_sel[:, :], 1.0).then_inc(pool_chain, 1)
            pool.memset(before[:, :, :], 1.0).then_inc(pool_chain, 1)
            count[0] += 3
            pool.wait_ge(pool_chain, count[0])
            pool.affine_select(out=ident[:, :], in_=ident[:, :], compare_op=ALU.not_equal, fill=1.0, base=0,
                               pattern=[[-1, P]], channel_multiplier=1).then_inc(consts_ready, 1)
            link(pool.affine_select(out=head_sel[:, :], in_=head_sel[:, :], compare_op=ALU.is_ge, fill=0.0, base=0,
                                    pattern=[[-DK, H]], channel_multiplier=1))
            pool.affine_select(out=head_sel[:, :], in_=head_sel[:, :], compare_op=ALU.is_ge, fill=0.0, base=DK - 1,
                               pattern=[[DK, H]], channel_multiplier=-1).then_inc(consts_ready, 1)
            pool.affine_select(out=before[:, :, :], in_=before[:, :, :], compare_op=ALU.is_gt, fill=0.0, base=0,
                               pattern=[[1, E], [-1, E]], channel_multiplier=0).then_inc(consts_ready, 1)
            pool.memset(ones[:, :], 1.0).then_inc(consts_ready, 1)
            pool.memset(v_tok[:, :, H * VW:VPAD], 0.0)
            v_heads = v_tok[:, :, 0:H * VW].rearrange("p t (h v) -> p t h v", v=VW)
            link(pool.memset(v_heads[:, :, :, DK], 1.0))
            pool.memset(q_ring[:, :, :, :].rearrange("p a b n -> p (a b n)").bitcast(U32), 0)
            link(pool.memset(k_ring[:, :, :, :].rearrange("p a b n -> p (a b n)").bitcast(U32), 0))
            pool.memset(k_ring[MROW:KROWS, :, :, :], 1.0).then_inc(ring_cleared, 1)
            pool.wait_ge(ring_cleared, 1)

            base = count[0]

            def split(w, i):
                g = w * 2 + i
                step = [0]

                def link_loop(ins):
                    step[0] += 1
                    ins.then_inc(pool_chain, 1)
                    pool.wait_ge(pool_chain, g * 4 + base + step[0])
                    pool.sem_inc(pool_gate, 1)

                pool.wait_ge(pT_copied, g + 1)
                pool.wait_ge(p_tr, g + 1)
                pool.wait_ge(parts_free, g - 1 + CREDIT)
                pool.sem_inc(pool_gate, 1)
                src = pT[:, i, :]
                link_loop(pool.tensor_copy(parts[:, i, 0, :], src))
                link_loop(pool.tensor_tensor(src, src, parts[:, i, 0, :], ALU.subtract))
                link_loop(pool.tensor_copy(parts[:, i, 1, :], src))
                pool.tensor_tensor(parts[:, i, 2, :], src, parts[:, i, 1, :], ALU.subtract).then_inc(parts_ready, 1)
                pool.wait_ge(n2_copied, g + 1)
                pool.wait_ge(parts_free, g + CREDIT)
                pool.sem_inc(pool_gate, 1)
                link_loop(pool.tensor_copy(m_blk[:, 0, :], m_half))
                pool.tensor_tensor(m_blk[:, 1, :], m_half, m_blk[:, 0, :], ALU.subtract).then_inc(m_ready, 1)

            with pool.Fori(0, NB // 2) as w:
                for i in range(2):
                    split(w, i)

            def load_values(w, i):
                pool.tensor_copy(v_ring[:, i, :, :],
                                 v_tok[:, bass.ds((w // 2) * KT, KT), bass.ds((w % 2) * (8 * VW) + 4 * VW * i, VSLOT)]
                                 ).then_inc(v_ready, 1)

            def store(w, i):
                pool.wait_ge(y_ready, w * 2 + i + 2)
                pool.dma_start(out_rows[bass.ds((w * 2 + i) * UT * P, UT * P), :].rearrange("(t p) d -> p t d", p=P),
                               y_sb[:, :, :]).then_inc(y_stored, 16)
                pool.wait_ge(y_stored, (w * 2 + i + 1) * 16)
                pool.sem_inc(y_free, 1)

            pool.wait_ge(p_copied, NB)
            pool.wait_ge(down_mm, NB * E + CREDIT)
            def step(w, first):
                for i in range(2):
                    pool.wait_ge(pv_done, (w * 2 + i - 1) * US + PV_CREDIT)
                    load_values(w, i)
                    if i == 1:
                        store(w, 0)
                    elif not first:
                        store(w - 1, 1)

            step(0, True)
            with pool.Fori(1, NU // 2) as w:
                step(w, False)
            store(NU // 2 - 1, 1)

        @block.scalar
        def _(act):
            act.wait_ge(wt_tr, 1)
            nc.scalar.copy(wvT[:, :], bank_m[0][:, 0:D])
            nc.scalar.copy(woT[:, :], bank_m[0][:, D:2 * D])
            nc.scalar.copy(cols[:, :], bank_m[0][:, 2 * D:2 * D + E * FC + 3]).then_inc(wt_copied, 1)
            act.wait_ge(wt_copied, 1)
            bv_col = cols[:, E * FC + 2:E * FC + 3]

            def prepare(g, slot, step, first=False):
                if step == 2:
                    act.wait_ge(xT_tr, g + 1)
                    if not first:
                        act.wait_ge(pT_mm, g)
                    nc.scalar.copy(xnT, bank_m[0][:, :]).then_inc(xT_copied, 1)
                elif step == 5:
                    act.wait_ge(router_d, g + 1)
                    nc.scalar.activation(ex[:, :, :], lg[:, :, :], ACT.Exp).then_inc(router_ex, 1)
                elif step == 6:
                    act.wait_ge(pT_mm, g + 1)
                    if not first:
                        act.wait_ge(n2_mm, g)
                    nc.scalar.activation(sqT[:, :], bank_m[0][:, :], ACT.Square, bias=bv_col).then_inc(sq_ready, 1)
                    act.wait_ge(parts_ready, g - 1 + CREDIT)
                    nc.scalar.activation(pT[:, slot, :], bank_m[0][:, :], ACT.Identity, bias=bv_col).then_inc(pT_copied, 1)
                elif step == 7:
                    act.wait_ge(n2_mm, g + 1)
                    nc.scalar.copy(n2T[:, bass.ds(g * BLK, BLK)], bank_m[1][0:H, :])
                    if not first:
                        act.wait_ge(m_ready, g)
                    nc.scalar.activation(m_half, bank_m[1][0:H, :], ACT.Copy, scale=-0.5).then_inc(n2_copied, 1)

            def experts(u, i, last=False):
                for e in range(E):
                    for c in range(FC):
                        act.wait_ge(up_mm, (u * E + e) * FC + c + 1)
                        act.wait_ge(down_mm, u * E + e - 1 + CREDIT)
                        nc.scalar.activation(hid[:, e % 2, c, :], pair[e % 2][:, c, :], ACT.Gelu,
                                             bias=cols[:, e * FC + c:e * FC + c + 1]).then_inc(gelu_done, 1)
                    if e == 1:
                        act.wait_ge(w_tr, u + 1)
                        nc.scalar.copy(wT[:, :], bank_m[0][0:E, :]).then_inc(wT_ready, 1)
                    if not last:
                        prepare(u + 1, 1 - i, e)

            for step in range(E):
                prepare(0, 0, step, True)
                if step == 3:
                    act.wait_ge(w1_in, 16)
                    for c in range(2):
                        some = slice(c * E // 2, (c + 1) * E // 2)
                        nc.scalar.copy(w1_parts[:, 0, some, :], w1_sb[:, some, :]).then_inc(w1_hi, 1)
            nc.scalar.activation(act_dummy[:, :], ones[:, 0:1], ACT.Gelu).then_inc(act_dummy_ready, 1)
            with act.Fori(0, NB // 2 - 1) as w:
                for i in range(2):
                    experts(w * 2 + i, i)
            experts(NB - 2, 0)
            experts(NB - 1, 1, last=True)
            for c in range(4):
                act.wait_ge(down_used, (c + 1) * NB // 4 * E + CREDIT)
                part = xn_tok[:, c * NT // 4:(c + 1) * NT // 4, :]
                nc.scalar.activation(part, part, ACT.Silu).then_inc(gate_ready, 1)
            act.wait_ge(act_dummy_ready, 1)
            nc.scalar.activation(act_dummy[:, :], act_dummy[:, :], ACT.Exp)
            with act.Fori(0, NU // 2) as w:
                for i in range(2):
                    for k in range(US):
                        for half in range(2):
                            act.wait_ge(scores_done, ((w * 2 + i) * US + k) * 2 + half + 1)
                            if half == 0:
                                act.wait_ge(pv_done, (w * 2 + i) * US + k + 1 - ES + PV_CREDIT)
                            nc.scalar.activation(exps[:, k % ES, 2 * half:2 * half + 2, :], pair[(2 * k + half) % 3][:, :, :], ACT.Exp,
                                                 scale=SCALE).then_inc(exp_done, 1)

        @block.vector
        def _(dve):
            NORM1 = -1
            NORM_LINKS = 5 + 3 * NEWTON
            ROUTER_LINKS = 11
            LINKS = 2 * NORM_LINKS + 1 + ROUTER_LINKS

            def tile(tensor, t):
                return tensor[:, bass.ds(t, 1), :].rearrange("p a d -> p (a d)")

            def prepare(g, slot, step):
                first = isinstance(g, int) and g == 0
                last = isinstance(g, int) and g == NB - 1
                at = {NORM1: 0 if first else -ROUTER_LINKS, 0: NORM_LINKS, 4: 2 * NORM_LINKS,
                      6: (2 if last else 3) * NORM_LINKS + 1}.get(step, 0)

                def link_block(ins):
                    nonlocal at
                    at += 1
                    ins.then_inc(dve_chain, 1)
                    dve.wait_ge(dve_chain, g * LINKS + at)

                if step == NORM1 or step == 0:
                    source, into, ready = ((lambda t: xn_blk[:, slot, t, :], z0_blk, z0_ready) if step == 0 else
                                           (lambda t: tile(x_tok, g * TB + t), xn_blk[:, slot], xn_ready))
                    for t in range(TB):
                        ins = nc.vector.bn_stats(stats[:, t, :], source(t))
                    link_block(ins)
                    dve.sem_inc(dve_gate, 1)
                    for t in range(TB):
                        ins = nc.vector.bn_aggr(mv[:, t, :], stats[:, t, :])
                    link_block(ins)
                    link_block(nc.vector.tensor_scalar(veps[:, :], mv[:, :, 1], EPS, None, ALU.add))
                    link_block(nc.vector.tensor_scalar(rstd[:, :].bitcast(I32), veps[:, :].bitcast(I32), 1, None,
                                                       ALU.logical_shift_right))
                    link_block(nc.vector.tensor_scalar(rstd[:, :].bitcast(I32), rstd[:, :].bitcast(I32), -1, RSQRT_SEED,
                                                       ALU.mult, ALU.add))
                    for _ in range(NEWTON):
                        link_block(nc.vector.scalar_tensor_tensor(out=newton[:, :], in0=rstd[:, :], scalar=-0.5,
                                                                  in1=rstd[:, :], op0=ALU.mult, op1=ALU.mult))
                        link_block(nc.vector.tensor_tensor(newton[:, :], newton[:, :], veps[:, :], ALU.mult))
                        link_block(nc.vector.scalar_tensor_tensor(out=rstd[:, :], in0=newton[:, :], scalar=1.5,
                                                                  in1=rstd[:, :], op0=ALU.add, op1=ALU.mult))
                    for t in range(TB):
                        ins = nc.vector.tensor_scalar(into[:, t, :], source(t), mv[:, t, 0:1], rstd[:, t:t + 1],
                                                      ALU.subtract, ALU.mult)
                    ins.then_inc(ready, 1)
                    dve.wait_ge(ready, g + 1)
                elif step == 3:
                    dve.wait_ge(zT_tr, g + 1)
                    nc.vector.tensor_scalar(zT[:, slot, :], bank_m[1][:, :], g_col, b_col, ALU.mult, ALU.add).then_inc(zT_ready, 1)
                    dve.wait_ge(zT_ready, g + 1)
                    nc.vector.tensor_copy(z_parts[:, slot, 0, :], zT[:, slot, :]).then_inc(z_hi, 1)
                    dve.wait_ge(z_hi, g + 1)
                    nc.vector.tensor_tensor(z_parts[:, slot, 1, :], zT[:, slot, :], z_parts[:, slot, 0, :].bitcast(F32),
                                            ALU.subtract).then_inc(z_split, 1)
                elif step == 4:
                    dve.wait_ge(logits_mm, g + 1)
                    nc.vector.tensor_tensor(lg[:, :, :], bank_m[1][:, 0:TB * E].rearrange("p (t e) -> p t e", e=E),
                                            rb_bc[:, :].unsqueeze(1).broadcast_to([P, TB, E]), ALU.add).then_inc(logits_used, 1)
                    dve.wait_ge(logits_used, g + 1)
                    link_block(nc.vector.tensor_reduce(red[:, :], lg[:, :, :], X, ALU.max))
                    nc.vector.tensor_tensor(lg[:, :, :], lg[:, :, :], red[:, :].unsqueeze(2).broadcast_to([P, TB, E]),
                                            ALU.subtract).then_inc(router_d, 1)
                elif step == 7:
                    dve.wait_ge(p_tr, g + 1)
                    v_heads = v_tok[:, bass.ds(g * TB, TB), 0:H * VW].rearrange("p t (h v) -> p t h v", v=VW)
                    nc.vector.tensor_copy(v_heads[:, :, :, 0:DK], bank_m[0][:, :].rearrange("p (t h d) -> p t h d", h=H, d=DK)
                                          ).then_inc(p_copied, 1)
                elif step == 6:
                    dve.wait_ge(router_d, g + 1)
                    other = lg[:, :, :].unsqueeze(2).broadcast_to([P, TB, E, E])
                    own = lg[:, :, :].unsqueeze(3).broadcast_to([P, TB, E, E])
                    nc.vector.tensor_tensor(cmp_gt[:, :, :, :], other, own, ALU.is_gt)
                    link_block(nc.vector.tensor_tensor(cmp_eq[:, :, :, :], other, own, ALU.is_equal))
                    link_block(nc.vector.tensor_tensor(cmp_eq[:, :, :, :], cmp_eq[:, :, :, :],
                                                       before[:, :, :].unsqueeze(1).broadcast_to([P, TB, E, E]), ALU.mult))
                    link_block(nc.vector.tensor_tensor(cmp_gt[:, :, :, :], cmp_gt[:, :, :, :], cmp_eq[:, :, :, :], ALU.add))
                    link_block(nc.vector.tensor_reduce(rank[:, :, :], cmp_gt[:, :, :, :], X, ALU.add))
                    dve.wait_ge(router_ex, g + 1)
                    link_block(nc.vector.tensor_reduce(red[:, :], ex[:, :, :], X, ALU.add))
                    link_block(nc.vector.reciprocal(red2[:, :], red[:, :]))
                    link_block(nc.vector.tensor_tensor(ex[:, :, :], ex[:, :, :],
                                                       red2[:, :].unsqueeze(2).broadcast_to([P, TB, E]), ALU.mult))
                    link_block(nc.vector.scalar_tensor_tensor(out=ex[:, :, :], in0=rank[:, :, :], scalar=1.5, in1=ex[:, :, :],
                                                              op0=ALU.is_lt, op1=ALU.mult))
                    link_block(nc.vector.tensor_reduce(red[:, :], ex[:, :, :], X, ALU.add))
                    link_block(nc.vector.tensor_scalar(red[:, :], red[:, :], 1e-8, None, ALU.max))
                    link_block(nc.vector.reciprocal(red2[:, :], red[:, :]))
                    nc.vector.tensor_tensor(w_blk[:, slot, :, :], ex[:, :, :], red2[:, :].unsqueeze(2).broadcast_to([P, TB, E]),
                                            ALU.mult).then_inc(router_done, 1)
                    assert at == (LINKS if last else LINKS + NORM_LINKS)


            def largest_by_head():
                dve.wait_ge(n2_copied, NB)
                nc.vector.tensor_reduce(max_head[:, :], n2T, X, ALU.max).then_inc(max_head_ready, 1)

            def largest():
                dve.wait_ge(max_head_tr, 1)
                nc.vector.tensor_reduce(m2[:, :], bank_m[0][0:1, 0:H], X, ALU.max).then_inc(m2_ready, 1)

            def experts(u, i, last=False, two_follow=False):
                if last:
                    largest_by_head()
                else:
                    prepare(u + 1, 1 - i, 0)
                dve.wait_ge(down_used, u * E + CREDIT)
                dve.wait_ge(bias_mm, u + 1)
                nc.vector.tensor_tensor(acc[:, :, :], bank_m[1][:, :].rearrange("p (t d) -> p t d", t=TB),
                                        xn_blk[:, i, :, :], ALU.add).then_inc(bias_used, 1)
                dve.wait_ge(router_done, u + 1)
                for e in range(E):
                    dve.wait_ge(down_mm, u * E + e + 1 + CREDIT)
                    if e == 0:
                        dve.wait_ge(bias_used, u + 1)
                    else:
                        dve.wait_ge(down_used, u * E + e + CREDIT)
                    for t in range(TB):
                        into = acc[:, t, :] if e < E - 1 else tile(xn_tok, u * TB + t)
                        ins = nc.vector.scalar_tensor_tensor(
                            out=into, in0=bank_o[e % 2][:, t * D:(t + 1) * D],
                            scalar=w_blk[:, i, t, e:e + 1], in1=acc[:, t, :], op0=ALU.mult, op1=ALU.add)
                    ins.then_inc(down_used, 1)
                    if not last and e + 2 < E:
                        prepare(u + 1, 1 - i, e + 2)
                    if e == 2 and two_follow:
                        prepare(u + 2, i, NORM1)
                    if last and e == 0:
                        largest()

            dve.wait_ge(x_in[0], 16)
            prepare(0, 0, NORM1)
            prepare(0, 0, 0)
            dve.wait_ge(wt_copied, 1)
            dve.wait_ge(small_in, 16 * 4)
            dve.wait_ge(consts_ready, 4)
            g_col = cols[:, E * FC:E * FC + 1]
            b_col = cols[:, E * FC + 1:E * FC + 2]
            prepare(0, 0, 3)
            for c in range(2):
                some = slice(c * E // 2, (c + 1) * E // 2)
                dve.wait_ge(w1_hi, c + 1)
                nc.vector.tensor_tensor(w1_parts[:, 1, some, :], w1_sb[:, some, :], w1_parts[:, 0, some, :].bitcast(F32),
                                        ALU.subtract).then_inc(w1_split, 1)
                if c == 0:
                    prepare(0, 0, 4)
                    prepare(1, 1, NORM1)
                    prepare(0, 0, 6)
                    prepare(0, 0, 7)
            for c in range(1, NT // XC):
                dve.wait_ge(x_in[c], 16)
            with dve.Fori(0, NB // 2 - 1) as w:
                for i in range(2):
                    experts(w * 2 + i, i, two_follow=True)
            experts(NB - 2, 0)
            experts(NB - 1, 1, last=True)
            link2_base = LINKS * NB
            for c in range(4):
                gate = xn_tok[:, c * NT // 4:(c + 1) * NT // 4, :]
                into = x_tok[:, c * NT // 4:(c + 1) * NT // 4, :]
                tmp = scratch[:, 0:N // 4].rearrange("p (t d) -> p t d", d=D)
                dve.wait_ge(gate_ready, c + 1)
                nc.vector.tensor_tensor(tmp, gate, bo_bc[:, :].unsqueeze(1).broadcast_to([P, NT // 4, D]),
                                        ALU.mult).then_inc(dve_chain, 1)
                dve.wait_ge(dve_chain, link2_base + 2 * c + 1)
                nc.vector.tensor_tensor(into, into, tmp, ALU.add).then_inc(dve_chain, 1)
                dve.wait_ge(dve_chain, link2_base + 2 * c + 2)
            base2 = link2_base + 8
            m2_bits = dve.value_load(m2[0:1, 0:1].bitcast(I32))
            with dve.If(m2_bits > M2_LIMIT_BITS):
                with dve.Fori(0, NU // 2) as w:
                    for i in range(2):
                        for k in range(US):
                            qh, kt = divmod(k, KT)
                            for half in range(2):
                                step = ((w * 2 + i) * US + k) * 2 + half
                                dve.wait_ge(exact_mm, step + 2)
                                into = row_max[:, bass.ds((w // 2) * KT + kt, 1), bass.ds((w % 2) * 8 + (4 * i + 2 * half), 2), qh]
                                nc.vector.tensor_reduce(into.rearrange("p t h -> p (t h)"), pair[half][:, :, :], X,
                                                        ALU.max).then_inc(exact_max, 1)
                dve.wait_ge(exact_max, NU * US * 2 + CREDIT)
                nc.vector.tensor_reduce(row_max2, row_max, X, ALU.max).then_inc(exact_max2, 1)
                dve.wait_ge(m_ready, NB)
                for g in range(NB):
                    dve.wait_ge(exact_tr, g + 1)
                    nc.vector.tensor_scalar(n2T[:, g * BLK:(g + 1) * BLK], bank_m[g % 2][0:H, :], -1.0, None,
                                            ALU.mult).then_inc(exact_neg, 1)
                dve.wait_ge(exact_neg, NB)
                nc.vector.tensor_copy(m_parts[:, 0, :], n2T).then_inc(exact_hi, 1)
                dve.wait_ge(exact_hi, 1)
                nc.vector.tensor_tensor(m_parts[:, 1, :], n2T, m_parts[:, 0, :], ALU.subtract).then_inc(exact_split, 1)
            per_unit = QH + 1
            with dve.Fori(0, NU // 2) as w:
                for i in range(2):
                    n = w * 2 + i
                    for qh in range(QH):
                        dve.wait_ge(pv_done, n * US + (qh + 1) * KT + PV_CREDIT)
                        nc.vector.transpose(o_turned[:, qh, :, :], bank_v[:, :].rearrange("p (r s) -> p s r", s=QR)
                                            ).then_inc(o_turned_ready, 1)
                        dve.wait_ge(o_turned_ready, n * QH + qh + 1 + CREDIT)
                        nc.vector.reciprocal(rden[:, qh, :], o_turned[:, qh, :, DK]).then_inc(dve_chain, 1)
                        dve.wait_ge(dve_chain, n * per_unit + base2 + qh + 1)
                        nc.vector.tensor_tensor(attn[:, qh, :, :], o_turned[:, qh, :, 0:DK],
                                                rden[:, qh, :].unsqueeze(2).broadcast_to([P, QR, DK]),
                                                ALU.mult).then_inc(attn_ready, 1)
                    dve.wait_ge(attn_tr, n + 1)
                    nc.vector.tensor_copy(attnT[:, :].rearrange("p (j a r) -> p a j r", j=4, a=QH),
                                          bank_f[:, 0:4 * RH].rearrange("p (a j r) -> p a j r", j=4, a=QH)
                                          ).then_inc(attnT_ready, 1)
                    dve.wait_ge(proj_done, n + 1)
                    dve.wait_ge(y_free, n + 1)
                    nc.vector.tensor_tensor(y_sb[:, :, :], bank_f[:, 0:UT * D].rearrange("p (t d) -> p t d", t=UT),
                                            xn_tok[:, bass.ds(n * UT, UT), :], ALU.mult).then_inc(dve_chain, 1)
                    dve.wait_ge(dve_chain, n * per_unit + base2 + per_unit)
                    nc.vector.tensor_tensor(y_sb[:, :, :], y_sb[:, :, :], x_tok[:, bass.ds(n * UT, UT), :],
                                            ALU.add).then_inc(y_ready, 1)

        @block.tensor
        def _(pe):
            pe.sem_inc(parts_ready, CREDIT)
            pe.sem_inc(parts_free, CREDIT)
            pe.sem_inc(down_mm, CREDIT)
            pe.sem_inc(down_used, CREDIT)
            pe.sem_inc(exp_done, CREDIT)
            pe.sem_inc(o_turned_ready, CREDIT)
            pe.sem_inc(y_ready, 1)
            pe.sem_inc(y_free, 1)
            pe.sem_inc(exact_mm, 1)
            pe.sem_inc(exact_max, CREDIT)
            pe.sem_inc(pv_done, PV_CREDIT)
            pe.wait_ge(consts_ready, 4)
            pe.wait_ge(rows_in, 16 * 6)
            nc.tensor.transpose(bank_m[0][:, 0:D], wv_sb[:, :], ident[:, :])
            nc.tensor.transpose(bank_m[0][:, D:2 * D], wo_sb[:, :], ident[:, :])
            R = E * FC + 3
            nc.tensor.transpose(bank_m[0][:, 2 * D:2 * D + R], rows[:, :], ident[0:R, 0:R]).then_inc(wt_tr, 1)
            pe.wait_ge(wt_copied, 1)
            pe.wait_ge(small_in, 16 * 4)

            def prepare(g, slot, step, first=False):
                if step == 2:
                    pe.wait_ge(xn_ready, g + 1)
                    for t in range(TB):
                        ins = nc.tensor.transpose(bank_m[0][:, t * P:(t + 1) * P], xn_blk[:, slot, t, :], ident[:, :])
                    ins.then_inc(xT_tr, 1)
                elif step == 3:
                    pe.wait_ge(z0_ready, g + 1)
                    if not first:
                        pe.wait_ge(bias_used, g)
                    for t in range(TB):
                        ins = nc.tensor.transpose(bank_m[1][:, t * P:(t + 1) * P], z0_blk[:, t, :], ident[:, :])
                    ins.then_inc(zT_tr, 1)
                elif step == 4:
                    pe.wait_ge(zT_ready, g + 1)
                    for t in range(TB):
                        ins = nc.tensor.matmul(bank_m[1][:, t * E:(t + 1) * E], zT[:, slot, t * P:(t + 1) * P], rw_sb[:, :],
                                               start=True, stop=True)
                    ins.then_inc(logits_mm, 1)
                elif step == 6:
                    pe.wait_ge(xT_copied, g + 1)
                    nc.tensor.matmul(bank_m[0][:, :], wvT[:, :], xnT, start=True, stop=True).then_inc(pT_mm, 1)
                elif step == 7:
                    pe.wait_ge(sq_ready, g + 1)
                    pe.wait_ge(pT_copied, g + 1)
                    for t in range(TB):
                        ins = nc.tensor.transpose(bank_m[0][:, t * D:(t + 1) * D], pT[:, slot, t * P:(t + 1) * P], ident[:, :])
                    ins.then_inc(p_tr, 1)
                    pe.wait_ge(logits_used, g + 1)
                    nc.tensor.matmul(bank_m[1][0:H, :], head_sel[:, :], sqT[:, :], start=True, stop=True).then_inc(n2_mm, 1)

            def experts(u, i, last=False):
                def up(e):
                    if e == E // 2:
                        pe.wait_ge(w1_split, 2)
                    for c in range(FC):
                        for k, (a, b) in enumerate(PRODUCTS):
                            ins = nc.tensor.matmul(pair[e % 2][:, c, :], w1_parts[:, a, e, c * P:(c + 1) * P],
                                                   z_parts[:, i, b, :], start=(k == 0), stop=(k == len(PRODUCTS) - 1))
                        ins.then_inc(up_mm, 1)

                def down(e):
                    pe.wait_ge(gelu_done, (u * E + e + 1) * FC)
                    pe.wait_ge(down_used, u * E + e - 1 + CREDIT)
                    for t in range(TB):
                        for c in range(FC):
                            ins = nc.tensor.matmul(bank_o[e % 2][:, t * D:(t + 1) * D], hid[:, e % 2, c, t * P:(t + 1) * P],
                                                   w2_sb[:, e, c, :], start=(c == 0), stop=(c == FC - 1))
                    ins.then_inc(down_mm, 1)

                pe.wait_ge(z_split, u + 1)
                for e in range(E):
                    if e >= 2:
                        down(e - 2)
                    up(e)
                    if e == 1:
                        pe.wait_ge(router_done, u + 1)
                        pe.wait_ge(p_copied, u + 1)
                        for t in range(TB):
                            ins = nc.tensor.transpose(bank_m[0][0:E, t * P:(t + 1) * P], w_blk[:, i, t, :], ident[:, :])
                        ins.then_inc(w_tr, 1)
                    elif e == 2:
                        pe.wait_ge(wT_ready, u + 1)
                        pe.wait_ge(n2_copied, u + 1)
                        for t in range(TB):
                            ins = nc.tensor.matmul(bank_m[1][:, t * D:(t + 1) * D], wT[:, t * P:(t + 1) * P], b2_sb[:, :],
                                                   start=True, stop=True)
                        ins.then_inc(bias_mm, 1)
                    if not last:
                        prepare(u + 1, 1 - i, e)
                    elif e == 3:
                        pe.wait_ge(max_head_ready, 1)
                        nc.tensor.transpose(bank_m[0][0:1, 0:H], max_head[:, :], ident[0:H, 0:H]).then_inc(max_head_tr, 1)
                down(E - 2)
                down(E - 1)

            for step in range(E):
                prepare(0, 0, step, True)
            pe.wait_ge(w1_split, 1)
            pe.wait_ge(w2_in, 16 * E)
            with pe.Fori(0, NB // 2 - 1) as w:
                for i in range(2):
                    experts(w * 2 + i, i)
            experts(NB - 2, 0)
            experts(NB - 1, 1, last=True)
            pe.wait_ge(down_used, NB * E + CREDIT)
            pe.wait_ge(m2_ready, 1)
            pe.wait_ge(bias_used, NB)
            m2_bits = pe.value_load(m2[0:1, 0:1].bitcast(I32))
            with pe.If(m2_bits > M2_LIMIT_BITS):
                with pe.Fori(0, NU // 2) as w:
                    for i in range(2):
                        pe.wait_ge(exact_in, (w * 2 + i + 1) * 16 * (KQ_LOADS - 1))
                        for k in range(US):
                            qh, kt = divmod(k, KT)
                            for half in range(2):
                                step = ((w * 2 + i) * US + k) * 2 + half
                                pe.wait_ge(exact_max, step - 1 + CREDIT)
                                for j in range(2 * half, 2 * half + 2):
                                    ins = nc.tensor.matmul(pair[half][:, j % 2, :], k_ring[0:PROWS, 0, j, kt * P:(kt + 1) * P],
                                                           q_ring[0:PROWS, 0, j, qh * BLK:(qh + 1) * BLK], start=True, stop=True)
                                ins.then_inc(exact_mm, 1)
                pe.wait_ge(exact_max2, 1)
                for g in range(NB):
                    if g >= 2:
                        pe.wait_ge(exact_neg, g - 1)
                    for t in range(TB):
                        ins = nc.tensor.transpose(bank_m[g % 2][0:H, t * P:(t + 1) * P], row_max2[:, g * TB + t, :], ident[:, :])
                    ins.then_inc(exact_tr, 1)
                pe.wait_ge(exact_split, 1)

            def scores(w, i, k, half):
                qh, kt = divmod(k, KT)
                n = w * 2 + i
                if k == 0 and half == 0:
                    pe.wait_ge(kq_in[i], (w + 1) * 16 * KQ_LOADS)
                h = 2 * k + half
                before_in_pair = h - 3 if h >= 3 else h - 2 if h < 2 else h - 5
                pe.wait_ge(exp_done, n * US * 2 + before_in_pair + 1 + CREDIT)
                for j in range(2 * half, 2 * half + 2):
                    ins = nc.tensor.matmul(pair[h % 3][:, j % 2, :], k_ring[0:KROWS, i, j, kt * P:(kt + 1) * P],
                                           q_ring[0:KROWS, i, j, qh * BLK:(qh + 1) * BLK], start=True, stop=True)
                ins.then_inc(scores_done, 1)

            def values(w, i, k):
                qh, kt = divmod(k, KT)
                n = w * 2 + i
                pe.wait_ge(exp_done, (n * US + k + 1) * 2 + CREDIT)
                if k == 0:
                    pe.wait_ge(v_ready, n + 1)
                if kt == 0:
                    pe.wait_ge(o_turned_ready, n * 2 + qh + CREDIT)
                for j in range(4):
                    ins = nc.tensor.matmul(bank_v[32 * j:32 * j + 32, :], v_ring[:, i, kt, VW * j:VW * j + 32],
                                           exps[:, k % ES, j, :], start=(kt == 0), stop=(kt == KT - 1))
                ins.then_inc(pv_done, 1)

            def finish(w, i, step):
                n = w * 2 + i
                if step == 0:
                    pe.wait_ge(attn_ready, (n + 1) * QH)
                    pe.wait_ge(y_ready, n + 1)
                    for a in range(QH):
                        ins = nc.tensor.transpose(bank_f[:, a * P:(a + 1) * P],
                                                  attn[:, a, :, :].rearrange("p q d -> p (q d)"), ident[:, :])
                    ins.then_inc(attn_tr, 1)
                else:
                    pe.wait_ge(attnT_ready, n + 1)
                    for t in range(UT):
                        ins = nc.tensor.matmul(bank_f[:, t * D:(t + 1) * D], attnT[:, t * P:(t + 1) * P], woT[:, :],
                                               start=True, stop=True)
                    ins.then_inc(proj_done, 1)

            def two_units(w, first):
                for g in range(2 * US):
                    i, k = divmod(g, US)
                    scores(w, i, k, 0)
                    if g >= VLAG:
                        values(w, *divmod(g - VLAG, US))
                    elif not first:
                        values(w - 1, 1, US + g - VLAG)
                    scores(w, i, k, 1)
                    if k - VLAG in FINISH_AT:
                        step = FINISH_AT.index(k - VLAG)
                        if i == 1:
                            finish(w, 0, step)
                        elif not first:
                            finish(w - 1, 1, step)

            VLAG = 2
            FINISH_AT = [1, 3]
            two_units(0, True)
            with pe.Fori(1, NU // 2) as w:
                two_units(w, False)
            for k in range(US - VLAG, US):
                values(NU // 2 - 1, 1, k)
            for step in range(len(FINISH_AT)):
                finish(NU // 2 - 1, 1, step)


_INS = ['L0_attn_x', 'L0_attn_Wv', 'L0_attn_bv', 'L0_attn_Wo', 'L0_attn_bo', 'L0_ffn_ln_g', 'L0_ffn_ln_b', 'L0_ffn_rW',
        'L0_ffn_rb', 'L0_ffn_W1', 'L0_ffn_b1', 'L0_ffn_W2', 'L0_ffn_b2']


def kernel(**inputs):
    import numpy as _np
    import concourse.bacc as _bacc
    from concourse.bass_utils import run_bass_kernel_spmd as _run

    nc = _bacc.Bacc("TRN2", target_bir_lowering=False, num_devices=1)
    arrays, args = {}, []
    for name in _INS:
        a = _np.ascontiguousarray(inputs[name])
        arrays[f"in_{name}"] = a
        args.append(nc.dram_tensor(f"in_{name}", a.shape, mybir.dt.from_np(a.dtype), kind="ExternalInput").ap())
    result = nc.dram_tensor("out_x", (B, S, D), F32, kind="ExternalOutput").ap()
    build(nc, *args, result)
    r = _run(nc, [arrays], core_ids=[0])
    return r.results[0]["out_x"]
```
